# Optimizing a Trainium2 kernel written in Bass

```python
import numpy as np
import jax
import jax.numpy as jnp

def _softmax(x, axis=-1):
    return jax.nn.softmax(x, axis=axis)

def _gelu(x):
    return jax.nn.gelu(x, approximate=True)

def _silu(x):
    return jax.nn.silu(x)

def _sigmoid(x):
    return jax.nn.sigmoid(x)

def _layernorm(x, axis=-1, eps=1e-05):
    m = jnp.mean(x, axis=axis, keepdims=True)
    v = jnp.var(x, axis=axis, keepdims=True)
    return (x - m) / jnp.sqrt(v + eps)

def _scatter_add(tgt, idx, src, axis=0):
    return tgt.at[idx].add(src)

def _segment_sum(src, seg, n):
    return jax.ops.segment_sum(src, seg, n)
kernel_name = 'mk_gnn_preln_d2_gnn_r8_8ed162'

def setup_inputs(seed: int=0):
    np.random.seed(seed)
    _w = jnp.asarray

    def _rec_inputs():
        import jax
        import jax.numpy as jnp
        _gk = jax.random.key(seed)
        x = -0.0005121 + 1.001 * jax.random.normal(jax.random.fold_in(_gk, 1), (12500, 32), jnp.float32)
        _s = jax.random.randint(jax.random.fold_in(_gk, 2), (200000,), 0, 12500, jnp.int32)
        _d = jax.random.randint(jax.random.fold_in(_gk, 3), (200000,), 0, 12500, jnp.int32)
        _loop = jnp.arange(12500, dtype=jnp.int32)
        src = jnp.concatenate([_s, _d, _loop])
        dst = jnp.concatenate([_d, _s, _loop])
        _o = jnp.argsort(dst, stable=True)
        src = src[_o]
        dst = dst[_o]
        edge_attr_4 = 0.00086875 + 0.999764 * jax.random.normal(jax.random.fold_in(_gk, 12), (412500, 4), jnp.float32)
        edge_attr_8 = jax.random.uniform(jax.random.fold_in(_gk, 13), (412500, 8), jnp.float32, 0.0, 1)
        return (x, src, dst, edge_attr_4, edge_attr_8)
    x, src, dst, edge_attr_4, edge_attr_8 = _rec_inputs()

    def _L0_gnn_setup():
        import jax, jax.numpy as jnp
        import numpy as np
        N = 12500
        E = 200000
        F_IN = 32
        F_OUT = 32
        key = jax.random.key(seed)
        k1, k2, k3, k4, k5 = jax.random.split(key, 5)
        x = jax.random.normal(k1, (N, F_IN), dtype=jnp.float32)
        edge_src = jax.random.randint(k2, (E,), 0, N, dtype=jnp.int32)
        edge_dst = jax.random.randint(k3, (E,), 0, N, dtype=jnp.int32)
        bound = 1.0 / np.sqrt(2 * F_IN)
        W = jax.random.uniform(k4, (2 * F_IN, F_OUT), minval=-bound, maxval=bound, dtype=jnp.float32)
        b = jax.random.uniform(k5, (F_OUT,), minval=-bound, maxval=bound, dtype=jnp.float32)
        return {'x': x, 'W': W, 'b': b, 'edge_src': edge_src, 'edge_dst': edge_dst}
    _L0_gnn_all = _L0_gnn_setup()
    _L0_gnn_in = {k: v for k, v in _L0_gnn_all.items() if k in ('W', 'b')}
    del _L0_gnn_all

    def _L1_gnn_setup():
        import jax, jax.numpy as jnp
        import numpy as np
        N = 4096
        E = 65536
        MUL = 8
        NB = 8
        HR = 64
        NTP = 4 * MUL * MUL
        AVG_NEI = 16.0
        INV_SQRT3 = 1.0 / np.sqrt(3.0)
        ALPHA = 1.0 / np.sqrt(2.0 * MUL)
        key = jax.random.key(seed)
        ks = jax.random.split(key, 12)
        h = jax.random.normal(ks[0], (N, 4 * MUL), jnp.float32)
        edge_index = jax.random.randint(ks[1], (2, E), 0, N)
        edge_sh = jax.random.normal(ks[2], (E, 4), jnp.float32)
        edge_radial = jax.random.uniform(ks[3], (E, NB), jnp.float32)

        def lin(k, fi, fo):
            return (jax.random.normal(k, (fi, fo), jnp.float32) / np.sqrt(fi)).astype(jnp.float32)
        W1 = lin(ks[4], NB, HR)
        b1 = jnp.zeros((HR,), jnp.float32)
        W2 = lin(ks[5], HR, HR)
        b2 = jnp.zeros((HR,), jnp.float32)
        W3 = lin(ks[6], HR, NTP)
        b3 = jnp.zeros((NTP,), jnp.float32)
        Ws = jax.random.normal(ks[7], (MUL, MUL), jnp.float32)
        Wv = jax.random.normal(ks[8], (MUL, MUL), jnp.float32)
        return dict(h=h, edge_index=edge_index, edge_sh=edge_sh, edge_radial=edge_radial, n_atoms=N, W1=W1, b1=b1, W2=W2, b2=b2, W3=W3, b3=b3, Ws=Ws, Wv=Wv)
    _L1_gnn_all = _L1_gnn_setup()
    _L1_gnn_in = {k: v for k, v in _L1_gnn_all.items() if k in ('W1', 'b1', 'W2', 'b2', 'W3', 'b3', 'Ws', 'Wv')}
    del _L1_gnn_all
    return {'x': x, 'src': src, 'dst': dst, 'edge_attr_4': edge_attr_4, 'edge_attr_8': edge_attr_8, 'L0_gnn_W': _L0_gnn_in['W'], 'L0_gnn_b': _L0_gnn_in['b'], 'L1_gnn_W1': _L1_gnn_in['W1'], 'L1_gnn_b1': _L1_gnn_in['b1'], 'L1_gnn_W2': _L1_gnn_in['W2'], 'L1_gnn_b2': _L1_gnn_in['b2'], 'L1_gnn_W3': _L1_gnn_in['W3'], 'L1_gnn_b3': _L1_gnn_in['b3'], 'L1_gnn_Ws': _L1_gnn_in['Ws'], 'L1_gnn_Wv': _L1_gnn_in['Wv']}

def reference(x, src, dst, edge_attr_4, edge_attr_8, L0_gnn_W, L0_gnn_b, L1_gnn_W1, L1_gnn_b1, L1_gnn_W2, L1_gnn_b2, L1_gnn_W3, L1_gnn_b3, L1_gnn_Ws, L1_gnn_Wv):
    import jax
    import jax.numpy as jnp

    def _L0_gnn_ref(x, W, b, edge_src, edge_dst):
        import jax, jax.numpy as jnp
        import numpy as np
        N = 12500
        E = 200000
        F_IN = 32
        F_OUT = 32
        n = x.shape[0]
        msgs = x[edge_src]
        summed = jax.ops.segment_sum(msgs, edge_dst, num_segments=n)
        cnt = jax.ops.segment_sum(jnp.ones_like(edge_dst, dtype=x.dtype), edge_dst, num_segments=n)
        neigh_mean = summed / jnp.maximum(cnt, 1.0)[:, None]
        h = jnp.concatenate([x, neigh_mean], axis=1)
        return jax.nn.relu(h @ W + b)

    def _L1_gnn_ref(h, edge_index, edge_sh, edge_radial, n_atoms, W1, b1, W2, b2, W3, b3, Ws, Wv):
        import jax, jax.numpy as jnp
        import numpy as np
        N = 4096
        E = 65536
        MUL = 8
        NB = 8
        HR = 64
        NTP = 4 * MUL * MUL
        AVG_NEI = 16.0
        INV_SQRT3 = 1.0 / np.sqrt(3.0)
        ALPHA = 1.0 / np.sqrt(2.0 * MUL)
        src, dst = (edge_index[0], edge_index[1])
        x = jax.nn.silu(edge_radial @ W1 + b1)
        x = jax.nn.silu(x @ W2 + b2)
        tpw = x @ W3 + b3
        P = MUL * MUL
        W00 = tpw[:, 0 * P:1 * P].reshape(-1, MUL, MUL)
        W110 = tpw[:, 1 * P:2 * P].reshape(-1, MUL, MUL)
        W01 = tpw[:, 2 * P:3 * P].reshape(-1, MUL, MUL)
        W10 = tpw[:, 3 * P:4 * P].reshape(-1, MUL, MUL)
        hs = h[:, :MUL]
        hv = h[:, MUL:].reshape(-1, MUL, 3)
        hs_e = hs[src]
        hv_e = hv[src]
        sh0 = edge_sh[:, 0]
        sh1 = edge_sh[:, 1:4]
        m0 = ALPHA * (jnp.einsum('eu,euw->ew', hs_e * sh0[:, None], W00) + INV_SQRT3 * jnp.einsum('eui,ei,euw->ew', hv_e, sh1, W110))
        m1 = ALPHA * (jnp.einsum('eu,ei,euw->ewi', hs_e, sh1, W01) + jnp.einsum('eui,euw->ewi', hv_e * sh0[:, None, None], W10))
        messages = jnp.concatenate([m0, m1.reshape(-1, 3 * MUL)], axis=-1)
        agg = jax.ops.segment_sum(messages, dst, num_segments=n_atoms) / np.sqrt(AVG_NEI)
        self0 = hs @ Ws / np.sqrt(MUL)
        self1 = jnp.einsum('nui,uw->nwi', hv, Wv) / np.sqrt(MUL)
        h_self = jnp.concatenate([self0, self1.reshape(-1, 3 * MUL)], axis=-1)
        return h_self + agg
    edge_index = jnp.stack([src, dst])
    h = jnp.maximum(_layernorm(x, axis=-1), 0.0)
    x = x + _L0_gnn_ref(h, L0_gnn_W, L0_gnn_b, src, dst)
    h = jnp.maximum(_layernorm(x, axis=-1), 0.0)
    x = x + _L1_gnn_ref(h, edge_index, edge_attr_4, edge_attr_8, 12500, L1_gnn_W1, L1_gnn_b1, L1_gnn_W2, L1_gnn_b2, L1_gnn_W3, L1_gnn_b3, L1_gnn_Ws, L1_gnn_Wv)
    return x

_drawn_inputs = setup_inputs


def setup_inputs(seed=0):
    import zlib

    import numpy as np

    out = dict(_drawn_inputs(seed))
    spreads = {'L1_gnn_b1': (0.0, 0.377), 'L1_gnn_b2': (0.0, 0.1), 'L1_gnn_b3': (0.0, 0.1)}
    factors = {}
    for name, (base, spread) in spreads.items():
        noise = np.random.default_rng([zlib.crc32(name.encode()), seed]).standard_normal(out[name].shape)
        drawn = base * np.exp(spread * noise) if base else spread * noise
        out[name] = jnp.asarray(drawn.astype(out[name].dtype))
    for name, factor in factors.items():
        out[name] = (out[name] * factor).astype(out[name].dtype)
    return out
```

```python
import concourse.bass as bass
from concourse import mybir
from contextlib import ExitStack

N = 12500
E = 412500
F = 32
MUL = 8
HR = 64
NB = 8
NTP = 4 * MUL * MUL
EPS = 1e-5

P = 128
C = 12
CHUNK = P * C
S = -(-E // CHUNK)
TWICE = S * CHUNK - E
MASKED = TWICE // C
assert TWICE % C == 0 and S % 2 == 1
PAIRS = C // 2
W = 56
NWIN = -(-N // W)
NPAD = N + W
GRP = 4
NG = C // GRP
TW = 6 * MUL * MUL

NP = 125
NJ = N // NP
QB = P // F
NQ = NJ // QB
JB = 15
JC = 16

K_ID, K_IOTA, K_COMB, K_THR = 0, P, P + W, P + W + 2 * F
K_ALL = K_THR + NWIN


def constants():
    import numpy as np
    k = np.zeros((P, K_ALL), np.float32)
    k[:, K_ID:K_ID + P] = np.eye(P)
    k[:, K_IOTA:K_IOTA + W] = np.arange(W)
    scale = 1.0 / np.sqrt(2.0 * MUL) / np.sqrt(16.0)
    for w in range(MUL):
        for u in range(MUL):
            k[w * MUL + u, K_COMB + w] = scale
            k[(MUL + w) * MUL + u, K_COMB + w] = scale / np.sqrt(3.0)
        for i in range(3):
            col = K_COMB + F + MUL + w * 3 + i
            k[MUL + i * MUL + w, col] = scale
            k[4 * MUL + i * MUL + w, col] = scale
    k[:, K_THR:] = np.arange(1, NWIN + 1) * W
    return k


def walk(eng, passes, step, at_start, at_end=None):
    even, odd = (S + 1) // 2, S // 2
    with eng.Fori(0, passes) as r:
        at_start(r)
        step(r=r, n=r * S, s=0, slot=0, use=r * even, then=r * odd)
        with eng.Fori(0, (S - 3) // 2) as i:
            step(r=r, n=r * S + i * 2 + 1, s=i * 2 + 1, slot=1, use=r * odd + i, then=r * even + i + 1)
            step(r=r, n=r * S + i * 2 + 2, s=i * 2 + 2, slot=0, use=r * even + i + 1, then=r * odd + i + 1)
        step(r=r, n=r * S + (S - 2), s=S - 2, slot=1, use=r * odd + (odd - 1), then=r * even + (even - 1))
        step(r=r, n=r * S + (S - 1), s=S - 1, slot=0, use=r * even + (even - 1), then=None)
        if at_end is not None:
            at_end(r)


def is_first(s):
    return isinstance(s, int) and s == 0


def is_last(s):
    return isinstance(s, int) and s == S - 1


def edges_of(s, a):
    if isinstance(s, int):
        rows = a[min(s * CHUNK, E - CHUNK):min(s * CHUNK, E - CHUNK) + CHUNK]
    else:
        rows = a[bass.ds(s * CHUNK, CHUNK)]
    if len(rows.shape) == 1:
        return rows.rearrange("(p c) -> p c", c=C)
    return rows.rearrange("(p c) k -> p (c k)", c=C)


def gnn(nc, x, src, dst, ea4, ea8, w0, b0, w1, b1, w2, b2, w3, b3, ws, wv, consts, out):
    f32, i32, bf16 = mybir.dt.float32, mybir.dt.int32, mybir.dt.bfloat16
    ALU, ACT, AX = mybir.AluOpType, mybir.ActivationFunctionType, mybir.AxisListType

    with ExitStack() as ctx:
        ctx.enter_context(nc.allow_non_contiguous_dma(reason="the small weights and tables, once"))

        def sb(name, shape, dt=f32):
            return ctx.enter_context(nc.sbuf_tensor(name, shape, dt))

        def sem(name):
            return ctx.enter_context(nc.semaphore(name))

        x_sb = sb("x_sb", [P, NJ, F])
        h_sb = sb("h_sb", [P, NJ, F])
        lin_sb = sb("lin_sb", [P, NJ, F])
        work = sb("work", [P, NJ * F])
        stat = sb("stat", [P, 3, NJ])
        rcount = sb("rcount", [P, NJ])
        hT = sb("hT", [P, 2, NP])
        agg_t = sb("agg_t", [P, NPAD])
        agg_m = sb("agg_m", [P, NPAD])
        dst_all = agg_t[:, 0:3 * CHUNK].bitcast(i32).rearrange("p (q e) -> p q e", q=3)
        low = sb("low", [P, 3])
        span = sb("span", [P, 3])
        base0 = sb("base0", [P, S])
        base = sb("base", [P, S])
        base_at = sb("base_at", [1, S], i32)
        span_row = sb("span_row", [1, 3 * P])
        over = sb("over", [1, NWIN])
        widest = sb("widest", [1, 2])
        npass = sb("npass", [1, 1], i32)
        src_sb = sb("src_sb", [P, 2, C], i32)
        dst_sb = sb("dst_sb", [P, 2, C], i32)
        sh_sb = sb("sh_sb", [P, 2, C, 4])
        rad_sb = sb("rad_sb", [P, 2, C * NB])
        local = sb("local", [P, C])
        onehot = sb("onehot", [P, 2, C, W])
        rows = sb("rows", [P, 2, C, 2 * F])
        radT = sb("radT", [C * NB, P])
        act1 = sb("act1", [P, 2, 3, P])
        act2 = sb("act2", [P, 2, PAIRS, P])
        coef = sb("coef", [P, 2, C, 3, MUL])
        coef_v = sb("coef_v", [P, 2, C, 3, MUL])
        dots = sb("dots", [P, C, MUL, 3])
        prod = work[:, 0:2 * GRP * TW].rearrange("p (a t k) -> p a t k", a=2, t=GRP)
        feat = sb("feat", [P, 2, GRP, 2 * F])
        k_sb = sb("k_sb", [P, K_ALL])
        ident = k_sb[:, K_ID:K_ID + P]
        w_self0 = sb("w_self0", [P, P])
        w_self1 = sb("w_self1", [P, P])
        w_mean = sb("w_mean", [P, F + 1])
        bias0 = sb("bias0", [P, F])
        w1_sb = sb("w1_sb", [C * NB, PAIRS, P])
        w2_sb = sb("w2_sb", [P, P])
        w3_raw = sb("w3_raw", [P, NTP])
        w3_sb = sb("w3_sb", [P, 2 * NTP])
        b1_sb = sb("b1_sb", [P, 1])
        b2_sb = sb("b2_sb", [P, 1])
        b3_raw = sb("b3_raw", [P, NTP])
        b3_rest = sb("b3_rest", [P, 3, NTP])
        b3_part = sb("b3_part", [P, NTP], bf16)
        b3_sb = sb("b3_sb", [P, 2, NTP], bf16)
        pick3 = sb("pick3", [P, P], bf16)

        ps = ctx.enter_context(nc.psum_tensor("ps", [P, 8, 512], f32))
        TPW, PS_M, PS_T, PS_IN, PS_H = 0, 4, 5, 6, 7

        h_dram = [nc.dram_tensor(f"h{k}_dram", [N, F], f32, kind="Internal").ap() for k in range(2)]
        low_dram = nc.dram_tensor("low_dram", [3 * P], f32, kind="Internal").ap()
        span_dram = nc.dram_tensor("span_dram", [3 * P], f32, kind="Internal").ap()

        zeroed, zeroed2 = sem("zeroed"), sem("zeroed2")
        x_in, k_in, weights_in, dst_in = sem("x_in"), sem("k_in"), sem("weights_in"), sem("dst_in")
        bias_parts, prep = sem("bias_parts"), sem("prep")
        spans, spans_out, spans_in = sem("spans"), sem("spans_out"), sem("spans_in")
        tables = sem("tables")
        norm, squared, rooted = sem("norm"), sem("squared"), sem("rooted")
        h_ready, h_out = sem("h_ready"), sem("h_out")
        turned, hT_ready, self_ready, self_used = sem("turned"), sem("hT_ready"), sem("self_ready"), sem("self_used")
        summed, node_step, out_ready, out_sent = sem("summed"), sem("node_step"), sem("out_ready"), sem("out_sent")
        pool_go = sem("pool_go")

        class Layer:
            def __init__(self, k):
                self.start = sem(f"start{k}")
                self.src_in = [sem(f"src_in{k}{a}") for a in range(2)]
                self.dst_in = [sem(f"dst_in{k}{a}") for a in range(2)]
                self.rad_in = [sem(f"rad_in{k}{a}") for a in range(2)]
                self.rows_in = [sem(f"rows_in{k}{a}") for a in range(2)]
                self.based = sem(f"based{k}")
                self.masked = sem(f"masked{k}")
                self.onehot = sem(f"onehot{k}")
                self.scattered = sem(f"scattered{k}")
                self.added = sem(f"added{k}")
                self.tick = sem(f"tick{k}")
                self.shifted = sem(f"shifted{k}")

        L0, L1 = Layer(0), Layer(1)
        turned_in, radT_done = sem("turned_in"), sem("radT_done")
        hid1, act1_done, hid2, act2_done = sem("hid1"), sem("act1_done"), sem("hid2"), sem("act2_done")
        scaled, dotted, coef_done = sem("scaled"), sem("dotted"), sem("coef_done")
        tpw, prod_a, prod_b, reduced, feats = sem("tpw"), sem("prod_a"), sem("prod_b"), sem("reduced"), sem("feats")

        block = ctx.enter_context(nc.Block())

        NW = 4 + 1 + 1 + 4 + 12 + 12 + 2 + 2 + 2 + 2 + 1

        @block.sync
        def _(sp):
            sp.dma_start(x_sb[0:NP], x.rearrange("(p j) f -> p j f", j=NJ)).then_inc(x_in, 16)
            sp.dma_start(k_sb[:], consts).then_inc(k_in, 16)
            sp.wait_ge(zeroed2, 1)
            full = 2 * P
            sp.dma_start(dst_all[:, 0:2], dst[0:full * CHUNK].rearrange("(q p e) -> p q e", q=2, e=CHUNK)).then_inc(dst_in, 16)
            sp.dma_start(dst_all[0:S - 1 - full, 2], dst[full * CHUNK:(S - 1) * CHUNK].rearrange("(p e) -> p e", e=CHUNK)).then_inc(dst_in, 16)
            sp.dma_start(dst_all[S - 1 - full:S - full, 2], dst[E - CHUNK:E].rearrange("(p e) -> p e", e=CHUNK)).then_inc(dst_in, 16)
            sp.wait_ge(zeroed, 1)
            for q in range(QB):
                sp.dma_start(w_self0[q * F:q * F + F, q * F:q * F + F], w0[0:F]).then_inc(weights_in, 16)
                sp.dma_start(w_self1[q * F:q * F + MUL, q * F:q * F + MUL], ws).then_inc(weights_in, 16)
                for i in range(3):
                    at = q * F + MUL + i
                    sp.dma_start(w_self1[at:at + 3 * MUL - 2:3, at:at + 3 * MUL - 2:3], wv).then_inc(weights_in, 16)
            sp.dma_start(w_mean[64:64 + F, 0:F], w0[F:2 * F]).then_inc(weights_in, 16)
            sp.dma_start(bias0[:], b0.unsqueeze(0).broadcast_to([P, F])).then_inc(weights_in, 16)
            for c in range(C):
                sp.dma_start(w1_sb[c * NB:c * NB + NB, c // 2, (c % 2) * HR:(c % 2) * HR + HR], w1).then_inc(weights_in, 16)
            for a in range(2):
                half = slice(a * HR, a * HR + HR)
                sp.dma_start(w2_sb[half, half], w2).then_inc(weights_in, 16)
                sp.dma_start(w3_raw[half], w3).then_inc(weights_in, 16)
                sp.dma_start(b1_sb[half], b1.unsqueeze(1)).then_inc(weights_in, 16)
                sp.dma_start(b2_sb[half], b2.unsqueeze(1)).then_inc(weights_in, 16)
            sp.dma_start(b3_raw[:], b3.unsqueeze(0).broadcast_to([P, NTP])).then_inc(weights_in, 16)
            sp.wait_ge(spans, 3)
            sp.dma_start(low_dram.rearrange("(q p) -> p q", q=3), low[:]).then_inc(spans_out, 16)
            sp.dma_start(span_dram.rearrange("(q p) -> p q", q=3), span[:]).then_inc(spans_out, 16)
            sp.wait_ge(spans_out, 32)
            sp.dma_start(base0[:], low_dram[0:S].unsqueeze(0).broadcast_to([P, S])).then_inc(spans_in, 16)
            sp.dma_start(span_row[:], span_dram.unsqueeze(0)).then_inc(spans_in, 16)
            sp.wait_ge(h_ready, 1)
            sp.dma_start(h_dram[0].rearrange("(p j) f -> p j f", j=NJ), h_sb[0:NP]).then_inc(h_out, 16)
            sp.wait_ge(tables, 1)
            passes = sp.value_load(npass[0:1, 0:1], min_val=1, max_val=NWIN)

            def load0(r, n, s, slot, use, then):
                sp.wait_ge(L0.added, n + 1)
                sp.dma_start(src_sb[:, slot], edges_of(s, src)).then_inc(L0.src_in[slot], 16)
                sp.dma_start(dst_sb[:, slot], edges_of(s, dst)).then_inc(L0.dst_in[slot], 16)
            walk(sp, passes, load0, lambda r: sp.wait_ge(L0.start, r + 1))

            sp.wait_ge(h_ready, 2)
            sp.dma_start(h_dram[1].rearrange("(p j) f -> p j f", j=NJ), h_sb[0:NP]).then_inc(h_out, 16)

            def load1(r, n, s, slot, use, then):
                sp.wait_ge(scaled, n + 1)
                sp.dma_start(src_sb[:, slot], edges_of(s, src)).then_inc(L1.src_in[slot], 16)
                sp.dma_start(rad_sb[:, slot], edges_of(s, ea8)).then_inc(L1.rad_in[slot], 16)
                sp.wait_ge(feats, n * NG + NG)
                sp.dma_start(dst_sb[:, slot], edges_of(s, dst)).then_inc(L1.dst_in[slot], 16)
                sp.dma_start(sh_sb[:, slot].rearrange("p c k -> p (c k)"), edges_of(s, ea4)).then_inc(L1.dst_in[slot], 16)
            walk(sp, passes, load1, lambda r: sp.wait_ge(L1.start, r + 1))

            for half in range(2):
                sp.wait_ge(out_ready, half + 1)
                js = slice(half * (NJ // 2), (half + 1) * (NJ // 2))
                sp.dma_start(out.rearrange("(p j) f -> p j f", j=NJ)[:, js], x_sb[0:NP, js]).then_inc(out_sent, 16)
            sp.wait_ge(out_sent, 32)

        @block.gpsimd
        def _(pool):
            pool.wait_ge(tables, 1)
            passes = pool.value_load(npass[0:1, 0:1], min_val=1, max_val=NWIN)
            for k, L in enumerate((L0, L1)):
                pool.wait_ge(h_out, 16 * (k + 1))
                pool.sem_inc(pool_go)

                def gather(r, n, s, slot, use, then):
                    pool.wait_ge(L.src_in[slot], use * 16 + 16)
                    pool.sem_inc(L.tick)
                    if k == 0:
                        pool.wait_ge(L.scattered, n + 1)
                        pool.sem_inc(L.tick)
                    else:
                        pool.wait_ge(scaled, n + 1)
                        pool.sem_inc(L.tick)
                        pool.wait_ge(dotted, n + 1)
                        pool.sem_inc(L.tick)
                    for c in range(C):
                        pool.indirect_dma_start(
                            out=rows[:, slot, c, 0:F], out_offset=None, in_=h_dram[k],
                            in_offset=bass.IndirectOffsetOnAxis(ap=src_sb[:, slot, c:c + 1], axis=0),
                            bounds_check=N - 1, oob_is_err=False).then_inc(L.rows_in[slot], 16)

                def start(r):
                    pool.wait_ge(L.start, r + 1)
                    pool.sem_inc(L.tick)
                walk(pool, passes, gather, start)

        @block.scalar
        def _(act):
            def norm_help(k):
                act.wait_ge(norm, 7 * k + 3)
                nc.scalar.activation(work[0:NP], h_sb[0:NP].rearrange("p j f -> p (j f)"), ACT.Square).then_inc(squared, 1)
                act.wait_ge(norm, 7 * k + 5)
                nc.scalar.activation(stat[0:NP, 2], stat[0:NP, 1], ACT.Sqrt).then_inc(rooted, 1)

            def self_help(k):
                for q in range(NQ):
                    act.wait_ge(turned, k * NQ + q + 1)
                    if q + k * NQ >= 2:
                        act.wait_ge(self_ready, k * NQ + q - 1)
                    nc.scalar.activation(hT[:, q % 2], ps[:, q % 2, 0:NP], ACT.Copy).then_inc(hT_ready, 1)

            norm_help(0)
            self_help(0)
            norm_help(1)
            self_help(1)
            act.sem_inc(scaled, 2)
            act.wait_ge(tables, 1)
            passes = act.value_load(npass[0:1, 0:1], min_val=1, max_val=NWIN)

            def mlp(m, slot):
                act.wait_ge(turned_in, m + 1)
                nc.scalar.activation(radT[:], ps[0:C * NB, PS_IN, 384:512], ACT.Copy).then_inc(radT_done, 1)
                for half in range(2):
                    act.wait_ge(hid1, m * 2 + (half + 1))
                    nc.scalar.activation(act1[:, half].rearrange("p q e -> p (q e)"), ps[:, PS_IN, 0:384], ACT.Silu,
                                         bias=b1_sb[:, 0:1]).then_inc(act1_done, 1)
                    act.wait_ge(hid2, m * 2 + (half + 1))
                    nc.scalar.activation(act2[:, slot, half * 3:half * 3 + 3].rearrange("p q e -> p (q e)"), ps[:, PS_H, 0:384],
                                         ACT.Silu, bias=b2_sb[:, 0:1]).then_inc(act2_done, 1)

            def start(r):
                act.wait_ge(L1.start, r + 1)
                mlp(r * S, 0)

            def scale(r, n, s, slot, use, then):
                act.wait_ge(L1.rows_in[slot], use * (16 * C) + 16 * C)
                act.wait_ge(L1.dst_in[slot], use * 32 + 32)
                act.wait_ge(prod_b, n * NG + NG)
                nc.scalar.activation(coef[:, slot, :, 2], rows[:, slot, :, 0:MUL], ACT.Copy)
                for c in range(C):
                    nc.scalar.activation(coef[:, slot, c, 0], rows[:, slot, c, 0:MUL], ACT.Copy,
                                         scale=sh_sb[:, slot, c, 0:1])
                    last_scale = nc.scalar.activation(
                        coef_v[:, slot, c], rows[:, slot, c, MUL:F].rearrange("p (u i) -> p i u", i=3), ACT.Copy,
                        scale=sh_sb[:, slot, c, 0:1])
                last_scale.then_inc(scaled, 1)
                if not is_last(s):
                    mlp(n + 1, 1 - slot)
            walk(act, passes, scale, start)

        @block.vector
        def _(dve):
            nc.vector.memset(dst_all[:, 2], 0).then_inc(zeroed2, 1)
            for t in (w_self0, w_self1, w_mean, w1_sb, w2_sb):
                nc.vector.memset(t[:], 0.0)
            nc.vector.memset(b3_sb[:], 0.0)
            nc.vector.memset(pick3[:], 0.0)
            nc.vector.memset(w3_sb[:], 0.0)
            nc.vector.memset(rows[:], 0.0)
            nc.vector.memset(feat[:], 0.0)
            nc.vector.memset(agg_m[:], 0.0).then_inc(zeroed, 1)
            dve.wait_ge(zeroed, 1)
            nc.vector.memset(rows[:, :, :, F:F + 1], 1.0)
            nc.vector.memset(w_mean[96:97, F:F + 1], 1.0)
            for a in range(3):
                last = nc.vector.memset(pick3[32 * a:32 * a + 1], 1.0)
            last.then_inc(zeroed, 1)
            dve.wait_ge(zeroed, 2)

            def layer_norm(k):
                xv, hv, n0 = x_sb[0:NP], h_sb[0:NP], 7 * k
                mean, var, root = (stat[0:NP, a] for a in range(3))
                nc.vector.tensor_reduce(mean, xv, AX.X, ALU.add).then_inc(norm, 1)
                dve.wait_ge(norm, n0 + 1)
                nc.vector.tensor_scalar(mean, mean, 1.0 / F, None, ALU.mult).then_inc(norm, 1)
                dve.wait_ge(norm, n0 + 2)
                nc.vector.tensor_tensor(hv, xv, mean.unsqueeze(2).broadcast_to([NP, NJ, F]), ALU.subtract).then_inc(norm, 1)
                dve.wait_ge(squared, k + 1)
                nc.vector.tensor_reduce(var, work[0:NP].rearrange("p (j f) -> p j f", f=F), AX.X, ALU.add).then_inc(norm, 1)
                dve.wait_ge(norm, n0 + 4)
                nc.vector.tensor_scalar(var, var, 1.0 / F, EPS, ALU.mult, ALU.add).then_inc(norm, 1)
                dve.wait_ge(rooted, k + 1)
                nc.vector.reciprocal(mean, root).then_inc(norm, 1)
                dve.wait_ge(norm, n0 + 6)
                nc.vector.tensor_tensor(hv, hv, mean.unsqueeze(2).broadcast_to([NP, NJ, F]), ALU.mult).then_inc(norm, 1)
                dve.wait_ge(norm, n0 + 7)
                nc.vector.tensor_scalar(hv, hv, 0.0, None, ALU.max).then_inc(h_ready, 1)

            def own_part(k):
                for q in range(NQ):
                    dve.wait_ge(self_ready, k * NQ + q + 1)
                    js = slice(q * QB, q * QB + QB)
                    got = ps[0:NP, 2 + q % 2, 0:P].rearrange("p (j f) -> p j f", f=F)
                    add = bias0[0:NP].unsqueeze(1).broadcast_to([NP, QB, F]) if k == 0 else x_sb[0:NP, js]
                    nc.vector.tensor_tensor(lin_sb[0:NP, js], got, add, ALU.add).then_inc(self_used, 1)

            dve.wait_ge(x_in, 16)
            layer_norm(0)

            dve.wait_ge(dst_in, 48)
            nc.vector.tensor_reduce(low[:], dst_all, AX.X, ALU.min).then_inc(spans, 1)
            nc.vector.tensor_reduce(span[:], dst_all, AX.X, ALU.max).then_inc(spans, 1)
            dve.wait_ge(spans, 2)
            nc.vector.tensor_tensor(span[:], span[:], low[:], ALU.subtract).then_inc(spans, 1)
            dve.wait_ge(spans_in, 32)
            nc.vector.tensor_reduce(widest[:, 0:1], span_row[:], AX.X, ALU.max).then_inc(prep, 1)
            dve.wait_ge(prep, 1)
            dve.wait_ge(k_in, 16)
            nc.vector.tensor_scalar(over[:], k_sb[0:1, K_THR:K_THR + NWIN], widest[:, 0:1], None, ALU.is_le).then_inc(prep, 1)
            dve.wait_ge(prep, 2)
            nc.vector.tensor_reduce(widest[:, 1:2], over[:], AX.X, ALU.add).then_inc(prep, 1)
            dve.wait_ge(prep, 3)
            nc.vector.tensor_scalar(npass[:], widest[:, 1:2], 1.0, None, ALU.add).then_inc(prep, 1)
            nc.vector.tensor_copy(base_at[:], base0[0:1]).then_inc(prep, 1)
            nc.vector.tensor_copy(base[:], base0[:]).then_inc(prep, 1)
            dve.wait_ge(prep, 6)
            nc.vector.memset(agg_t[:], 0.0).then_inc(tables, 1)

            dve.wait_ge(weights_in, 16 * NW)
            nc.vector.tensor_scalar(w_self1[:], w_self1[:], MUL ** -0.5, None, ALU.mult).then_inc(prep, 1)
            for a in range(2):
                half = slice(a * HR, a * HR + HR)
                nc.vector.tensor_copy(
                    w3_sb[half, a * NTP:(a + 1) * NTP].rearrange("p (g w u) -> p g w u", g=4, w=MUL),
                    w3_raw[half].rearrange("p (g u w) -> p g w u", g=4, w=MUL)).then_inc(prep, 1)
            nc.vector.tensor_copy(b3_rest[:, 0].rearrange("p (g w u) -> p g w u", g=4, w=MUL),
                                  b3_raw[:].rearrange("p (g u w) -> p g w u", g=4, w=MUL)).then_inc(bias_parts, 1)
            dve.wait_ge(bias_parts, 1)
            for a in range(3):
                nc.vector.tensor_copy(b3_part[:], b3_rest[:, a]).then_inc(bias_parts, 1)
                dve.wait_ge(bias_parts, 2 + 4 * a)
                row = slice(32 * a, 32 * a + 1)
                nc.vector.tensor_copy(b3_sb[row, 0], b3_part[row]).then_inc(bias_parts, 1)
                nc.vector.tensor_copy(b3_sb[row, 1], b3_part[row]).then_inc(bias_parts, 1)
                nc.vector.tensor_tensor(b3_rest[:, (a + 1) % 3], b3_rest[:, a], b3_part[:], ALU.subtract).then_inc(bias_parts, 1)
                dve.wait_ge(bias_parts, 5 + 4 * a)
            own_part(0)

            passes = dve.value_load(npass[0:1, 0:1], min_val=1, max_val=NWIN)
            iota = k_sb[:, K_IOTA:K_IOTA + W].unsqueeze(1).broadcast_to([P, C, W])

            def one_hot(L, r, n, s, slot):
                start = base[:, s:s + 1] if isinstance(s, int) else base[:, bass.ds(s, 1)]
                nc.vector.tensor_tensor(local[:], dst_sb[:, slot], start.broadcast_to([P, C]), ALU.subtract).then_inc(L.based, 1)
                dve.wait_ge(L.based, n + 1)
                if is_last(s):
                    nc.vector.memset(local[0:MASKED], -1.0).then_inc(L.masked, 1)
                    dve.wait_ge(L.masked, r + 1)
                nc.vector.tensor_tensor(onehot[:, slot], iota, local[:].unsqueeze(2).broadcast_to([P, C, W]),
                                        ALU.is_equal).then_inc(L.onehot, 1)

            def window(s):
                at = base_at[0:1, s:s + 1] if isinstance(s, int) else base_at[0:1, bass.ds(s, 1)]
                return dve.value_load(at, min_val=0, max_val=N)

            def next_windows(L, each, credit):
                def at_end(r):
                    dve.wait_ge(L.added, (r + 1) * (S * each) + credit)
                    nc.vector.tensor_scalar(base[:], base[:], float(W), None, ALU.add).then_inc(L.shifted, 1)
                    dve.wait_ge(L.shifted, r * 2 + 1)
                    nc.vector.tensor_scalar(base_at[:], base[0:1], float(N), None, ALU.min).then_inc(L.shifted, 1)
                    dve.wait_ge(L.shifted, r * 2 + 2)
                    dve.sem_inc(L.start)
                return at_end

            dve.sem_inc(L0.added, 2)
            dve.sem_inc(L0.start)

            def sum_rows(r, n, s, slot, use, then):
                dve.wait_ge(L0.dst_in[slot], use * 16 + 16)
                dve.wait_ge(L0.scattered, n + 1)
                one_hot(L0, r, n, s, slot)
                at = window(s)
                dve.wait_ge(L0.scattered, n + 3)
                dve.wait_ge(L0.added, n + 2)
                cols = agg_m[64:128, bass.ds(at, W)]
                nc.vector.tensor_tensor(cols, cols, ps[64:128, slot, 0:W], ALU.add).then_inc(L0.added, 1)
            walk(dve, passes, sum_rows, lambda r: None, next_windows(L0, 1, 2))

            nb = -(-NJ // JB)
            for b in range(nb):
                js = slice(b * JB, min(NJ, b * JB + JB))
                wide = js.stop - js.start
                got = ps[0:NP, b, 0:wide * (F + 1)].rearrange("p (j f) -> p j f", f=F + 1)
                if b == 0:
                    dve.wait_ge(h_out, 16)
                    nc.vector.tensor_copy(base_at[:], base0[0:1])
                    nc.vector.tensor_copy(base[:], base0[:]).then_inc(prep, 1)
                dve.wait_ge(summed, b + 1)
                nc.vector.tensor_scalar(rcount[0:NP, js], got[:, :, F], 1.0, None, ALU.max).then_inc(node_step, 1)
                dve.wait_ge(node_step, 5 * b + 1)
                nc.vector.reciprocal(rcount[0:NP, js], rcount[0:NP, js]).then_inc(node_step, 1)
                dve.wait_ge(node_step, 5 * b + 2)
                h = h_sb[0:NP, js]
                nc.vector.tensor_tensor(h, got[:, :, 0:F], rcount[0:NP, js].unsqueeze(2).broadcast_to([NP, wide, F]),
                                        ALU.mult).then_inc(node_step, 1)
                dve.wait_ge(node_step, 5 * b + 3)
                nc.vector.tensor_tensor(h, h, lin_sb[0:NP, js], ALU.add).then_inc(node_step, 1)
                dve.wait_ge(node_step, 5 * b + 4)
                nc.vector.scalar_tensor_tensor(out=x_sb[0:NP, js], in0=h, scalar=0.0, in1=x_sb[0:NP, js],
                                               op0=ALU.max, op1=ALU.add).then_inc(node_step, 1)
            dve.wait_ge(node_step, 5 * nb)
            layer_norm(1)
            own_part(1)
            dve.wait_ge(prep, 10)

            dve.sem_inc(feats, 2 * NG)
            dve.sem_inc(prod_b, 2 * NG)
            dve.sem_inc(dotted, 2)
            dve.sem_inc(L1.added, 1)
            dve.sem_inc(L1.start)

            def add_window(n_added, at):
                dve.wait_ge(L1.added, n_added * 2 + 1)
                for rows_, agg, bank in ((P, agg_t, PS_T), (64, agg_m, PS_M)):
                    cols = agg[0:rows_, bass.ds(at, W)]
                    nc.vector.tensor_tensor(cols, cols, ps[0:rows_, bank, 0:W], ALU.add).then_inc(L1.added, 1)

            def products(r, n, s, slot, use, then):
                before = None if is_first(s) else window(s - 1)
                here = window(s) if is_last(s) else None
                dve.wait_ge(L1.dst_in[slot], use * 32 + 32)
                one_hot(L1, r, n, s, slot)
                dve.wait_ge(L1.rows_in[slot], use * (16 * C) + 16 * C)
                nc.vector.tensor_tensor(
                    dots[:], rows[:, slot, :, MUL:F].rearrange("p c (u i) -> p c u i", i=3),
                    sh_sb[:, slot, :, 1:4].unsqueeze(2).broadcast_to([P, C, MUL, 3]), ALU.mult).then_inc(dotted, 1)
                dve.wait_ge(dotted, n + 3)
                nc.vector.tensor_reduce(coef[:, slot, :, 1], dots[:], AX.X, ALU.add).then_inc(coef_done, 1)
                dve.wait_ge(coef_done, n + 1)
                dve.wait_ge(scaled, n + 3)
                for g in range(NG):
                    a = (slot + g) % 2
                    m = n * NG + g
                    ts = slice(g * GRP, g * GRP + GRP)
                    dve.wait_ge(tpw, m + 1)
                    dve.wait_ge(L1.scattered, m + 1)
                    t4 = ps[:, TPW + 2 * a:TPW + 2 * a + 2].rearrange("p b (t k) -> p (b t) k", k=NTP)
                    nc.vector.tensor_tensor(
                        prod[:, a, :, 0:192].rearrange("p t (g w u) -> p t g w u", g=3, w=MUL),
                        t4[:, :, 0:192].rearrange("p t (g w u) -> p t g w u", g=3, w=MUL),
                        coef[:, slot, ts].unsqueeze(3).broadcast_to([P, GRP, 3, MUL, MUL]), ALU.mult).then_inc(prod_a, 1)
                    nc.vector.tensor_tensor(
                        prod[:, a, :, 192:384].rearrange("p t (i w u) -> p t i w u", i=3, w=MUL),
                        t4[:, :, 192:256].rearrange("p t (w u) -> p t w u", w=MUL).unsqueeze(2).broadcast_to([P, GRP, 3, MUL, MUL]),
                        coef_v[:, slot, ts].unsqueeze(3).broadcast_to([P, GRP, 3, MUL, MUL]), ALU.mult).then_inc(prod_b, 1)
                    if g == 0 and not is_first(s):
                        dve.wait_ge(L1.scattered, m + 2)
                        add_window(n - 1, before)
                    dve.wait_ge(prod_a, m + 1)
                    dve.wait_ge(prod_b, m + 1 + 2 * NG)
                    nc.vector.tensor_reduce(
                        feat[:, a, :, 0:4 * MUL], prod[:, a, :, 128:384].rearrange("p t (k u) -> p t k u", u=MUL),
                        AX.X, ALU.add).then_inc(reduced, 1)
                    dve.wait_ge(reduced, m + 1)
                    nc.vector.tensor_tensor(
                        feat[:, a, :, 4 * MUL:7 * MUL].rearrange("p t (i w) -> p t i w", i=3),
                        feat[:, a, :, 0:MUL].unsqueeze(2).broadcast_to([P, GRP, 3, MUL]),
                        sh_sb[:, slot, ts, 1:4].unsqueeze(3).broadcast_to([P, GRP, 3, MUL]), ALU.mult).then_inc(feats, 1)
                if is_last(s):
                    dve.wait_ge(L1.scattered, n * NG + NG + 2)
                    add_window(n, here)
            walk(dve, passes, products, lambda r: None, next_windows(L1, 2, 1))

            nb = -(-NJ // JC)
            dve.wait_ge(self_used, 2 * NQ)
            for b in range(nb):
                js = slice(b * JC, min(NJ, b * JC + JC))
                wide = js.stop - js.start
                dve.wait_ge(summed, -(-NJ // JB) + b + 1)
                ins = nc.vector.tensor_tensor(x_sb[0:NP, js], ps[0:NP, b, 0:wide * F].rearrange("p (j f) -> p j f", f=F),
                                              lin_sb[0:NP, js], ALU.add)
                if b in (3, nb - 1):
                    ins.then_inc(out_ready, 1)

        @block.tensor
        def _(pe):
            pe.wait_ge(k_in, 16)
            pe.wait_ge(weights_in, 16 * NW)
            pe.wait_ge(zeroed, 2)

            def own_part(k):
                wt = w_self0 if k == 0 else w_self1

                def product(q):
                    pe.wait_ge(hT_ready, k * NQ + q + 1)
                    if k * NQ + q >= 2:
                        pe.wait_ge(self_used, k * NQ + q - 1)
                    nc.tensor.matmul(ps[0:NP, 2 + q % 2, 0:P], hT[:, q % 2], wt[:], start=True, stop=True).then_inc(self_ready, 1)

                pe.wait_ge(h_ready, k + 1)
                for q in range(NQ):
                    if q >= 2:
                        pe.wait_ge(hT_ready, k * NQ + q - 1)
                    nc.tensor.transpose(ps[:, q % 2, 0:NP], h_sb[0:NP, q * QB:q * QB + QB].rearrange("p j f -> p (j f)"),
                                        k_sb[0:NP, K_ID:K_ID + NP]).then_inc(turned, 1)
                    if q >= 1:
                        product(q - 1)
                product(NQ - 1)

            own_part(0)
            pe.sem_inc(L0.scattered, 2)
            pe.wait_ge(tables, 1)
            passes = pe.value_load(npass[0:1, 0:1], min_val=1, max_val=NWIN)
            pe.wait_ge(self_used, NQ)

            def sum_rows(r, n, s, slot, use, then):
                pe.wait_ge(L0.rows_in[slot], use * (16 * C) + 16 * C)
                pe.wait_ge(L0.onehot, n + 1)
                pe.wait_ge(L0.added, n + 1)
                for c in range(C):
                    ins = nc.tensor.matmul(ps[64:128, slot, 0:W], rows[:, slot, c], onehot[:, slot, c],
                                           start=(c == 0), stop=(c == C - 1))
                ins.then_inc(L0.scattered, 1)
            walk(pe, passes, sum_rows, lambda r: pe.wait_ge(L0.start, r + 1))

            pe.wait_ge(L0.start, passes + 1)
            for b in range(-(-NJ // JB)):
                for j in range(b * JB, min(NJ, b * JB + JB)):
                    at = (j - b * JB) * (F + 1)
                    ins = nc.tensor.matmul(ps[0:NP, b, at:at + F + 1], agg_m[64:128, j:j + NJ * (NP - 1) + 1:NJ],
                                           w_mean[64:128], start=True, stop=True)
                ins.then_inc(summed, 1)
            pe.wait_ge(prep, 9)
            own_part(1)
            pe.wait_ge(self_used, 2 * NQ)
            pe.sem_inc(L1.scattered, 2)
            pe.wait_ge(bias_parts, 13)

            def turn_in(m, slot, use):
                pe.wait_ge(L1.rad_in[slot], use * 16 + 16)
                nc.tensor.transpose(ps[0:C * NB, PS_IN, 384:512], rad_sb[:, slot], ident).then_inc(turned_in, 1)

            def hidden1(m, half):
                if half == 0:
                    pe.wait_ge(radT_done, m + 1)
                else:
                    pe.wait_ge(act1_done, m * 2 + 1)
                for q in range(3):
                    ins = nc.tensor.matmul(ps[:, PS_IN, q * P:q * P + P], w1_sb[:, half * 3 + q], radT[:], start=True, stop=True)
                ins.then_inc(hid1, 1)

            def hidden2(m, half):
                pe.wait_ge(act1_done, m * 2 + half + 1)
                if half == 1:
                    pe.wait_ge(act2_done, m * 2 + 1)
                nc.tensor.matmul(ps[:, PS_H, 0:3 * P], w2_sb[:], act1[:, half].rearrange("p q e -> p (q e)"),
                                 start=True, stop=True).then_inc(hid2, 1)

            def weights(n, g, slot):
                a = (slot + g) % 2
                pe.wait_ge(act2_done, n * 2 + 2)
                pe.wait_ge(prod_b, n * NG + (2 * NG - 1 + g))
                for b in range(2):
                    bank = ps[:, TPW + 2 * a + b]
                    nc.tensor.matmul(bank, pick3[:], b3_sb[:].rearrange("p a k -> p (a k)"), start=True, stop=False)
                    ins = nc.tensor.matmul(bank, act2[:, slot, 2 * g + b], w3_sb[:], start=False, stop=True)
                ins.then_inc(tpw, 1)

            def scatter(n, g, slot):
                a = (slot + g) % 2
                if g == 0:
                    pe.wait_ge(L1.onehot, n + 1)
                pe.wait_ge(feats, n * NG + g + 1 + 2 * NG)
                if g == 0:
                    pe.wait_ge(L1.added, n * 2 + 1)
                for t in range(GRP):
                    c = g * GRP + t
                    flags = dict(start=(c == 0), stop=(c == C - 1))
                    nc.tensor.matmul(ps[:, PS_T, 0:W], prod[:, a, t, 0:P], onehot[:, slot, c], **flags)
                    ins = nc.tensor.matmul(ps[0:64, PS_M, 0:W], feat[:, a, t], onehot[:, slot, c], **flags)
                ins.then_inc(L1.scattered, 1)

            def start(r):
                pe.wait_ge(L1.start, r + 1)
                m = r * S
                turn_in(m, 0, r * ((S + 1) // 2))
                for half in range(2):
                    hidden1(m, half)
                    hidden2(m, half)

            def group_steps(r, n, s, slot, use, then):
                m, other, last = n + 1, 1 - slot, is_last(s)
                weights(n, 0, slot)
                weights(n, 1, slot)
                if not last:
                    turn_in(m, other, then)
                    hidden1(m, 0)
                scatter(n, 0, slot)
                weights(n, 2, slot)
                if not last:
                    hidden2(m, 0)
                    hidden1(m, 1)
                scatter(n, 1, slot)
                if not last:
                    hidden2(m, 1)
                scatter(n, 2, slot)

            walk(pe, passes, group_steps, start)

            pe.wait_ge(L1.start, passes + 1)
            for b in range(-(-NJ // JC)):
                for j in range(b * JC, min(NJ, b * JC + JC)):
                    at = (j - b * JC) * F
                    cols = slice(j, j + NJ * (NP - 1) + 1, NJ)
                    nc.tensor.matmul(ps[0:NP, b, at:at + F], agg_t[:, cols], k_sb[:, K_COMB:K_COMB + F], start=True, stop=False)
                    ins = nc.tensor.matmul(ps[0:NP, b, at:at + F], agg_m[0:64, cols], k_sb[0:64, K_COMB + F:K_COMB + 2 * F],
                                           start=False, stop=True)
                ins.then_inc(summed, 1)


_INS = ['x', 'src', 'dst', 'edge_attr_4', 'edge_attr_8', 'L0_gnn_W', 'L0_gnn_b', 'L1_gnn_W1', 'L1_gnn_b1', 'L1_gnn_W2',
        'L1_gnn_b2', 'L1_gnn_W3', 'L1_gnn_b3', 'L1_gnn_Ws', 'L1_gnn_Wv']


def kernel(**inputs):
    import numpy as np
    import concourse.bacc as bacc
    from concourse.bass_utils import run_bass_kernel_spmd

    nc = bacc.Bacc("TRN2", target_bir_lowering=False, num_devices=1)
    arrays, args = {}, []
    for name in _INS:
        arrays[f"in_{name}"] = np.ascontiguousarray(inputs[name])
    arrays["in_constants"] = constants()
    for name, a in arrays.items():
        args.append(nc.dram_tensor(name, a.shape, mybir.dt.from_np(a.dtype), kind="ExternalInput").ap())
    args.append(nc.dram_tensor("out_x", (N, F), mybir.dt.float32, kind="ExternalOutput").ap())
    gnn(nc, *args)
    result = run_bass_kernel_spmd(nc, [arrays], core_ids=[0])
    return result.results[0]["out_x"]
```

```python
import concourse.bass as bass
from concourse import mybir
from contextlib import ExitStack

N = 12500
E = 412500
F = 32
MUL = 8
HR = 64
NB = 8
NTP = 4 * MUL * MUL
EPS = 1e-5

P = 128
C = 12
CHUNK = P * C
S = -(-E // CHUNK)
TWICE = S * CHUNK - E
MASKED = TWICE // C
assert TWICE % C == 0 and S % 2 == 1
PAIRS = C // 2
W = 56
NWIN = -(-N // W)
NPAD = N + W
GRP = 4
NG = C // GRP
B = MUL * MUL
TW = 7 * B

NP = 125
NJ = N // NP
QB = P // F
NQ = NJ // QB
JB = 15
JC = 16

K_ID, K_IOTA, K_COMB, K_THR = 0, P, P + W, P + W + 2 * F
K_ALL = K_THR + NWIN


def constants():
    import numpy as np
    k = np.zeros((P, K_ALL), np.float32)
    k[:, K_ID:K_ID + P] = np.eye(P)
    k[:, K_IOTA:K_IOTA + W] = np.arange(W)
    scale = 1.0 / np.sqrt(2.0 * MUL) / np.sqrt(16.0)
    for w in range(MUL):
        for i in range(3):
            col = K_COMB + F + MUL + w * 3 + i
            if i > 0:
                k[(i - 1) * MUL + w, col] = scale
            k[(3 + i) * MUL + w, col] = scale
        for u in range(MUL):
            k[w * MUL + u, K_COMB + w] = scale
            k[B + w * MUL + u, K_COMB + w] = scale / np.sqrt(3.0)
            k[B + w * MUL + u, K_COMB + F + MUL + w * 3] = scale
    k[:, K_THR:] = np.arange(1, NWIN + 1) * W
    return k


def walk(eng, passes, step, at_start, at_end=None):
    even, odd = (S + 1) // 2, S // 2
    with eng.Fori(0, passes) as r:
        at_start(r)
        step(r=r, n=r * S, s=0, slot=0, use=r * even, then=r * odd)
        with eng.Fori(0, (S - 3) // 2) as i:
            step(r=r, n=r * S + i * 2 + 1, s=i * 2 + 1, slot=1, use=r * odd + i, then=r * even + i + 1)
            step(r=r, n=r * S + i * 2 + 2, s=i * 2 + 2, slot=0, use=r * even + i + 1, then=r * odd + i + 1)
        step(r=r, n=r * S + (S - 2), s=S - 2, slot=1, use=r * odd + (odd - 1), then=r * even + (even - 1))
        step(r=r, n=r * S + (S - 1), s=S - 1, slot=0, use=r * even + (even - 1), then=None)
        if at_end is not None:
            at_end(r)


def is_first(s):
    return isinstance(s, int) and s == 0


def is_last(s):
    return isinstance(s, int) and s == S - 1


def edges_of(s, a):
    if isinstance(s, int):
        rows = a[min(s * CHUNK, E - CHUNK):min(s * CHUNK, E - CHUNK) + CHUNK]
    else:
        rows = a[bass.ds(s * CHUNK, CHUNK)]
    if len(rows.shape) == 1:
        return rows.rearrange("(p c) -> p c", c=C)
    return rows.rearrange("(p c) k -> p (c k)", c=C)


def gnn(nc, x, src, dst, ea4, ea8, w0, b0, w1, b1, w2, b2, w3, b3, ws, wv, consts, out):
    f32, i32, bf16 = mybir.dt.float32, mybir.dt.int32, mybir.dt.bfloat16
    ALU, ACT, AX = mybir.AluOpType, mybir.ActivationFunctionType, mybir.AxisListType

    with ExitStack() as ctx:
        ctx.enter_context(nc.allow_non_contiguous_dma(reason="the small weights and tables, once"))

        def sb(name, shape, dt=f32):
            return ctx.enter_context(nc.sbuf_tensor(name, shape, dt))

        def sem(name):
            return ctx.enter_context(nc.semaphore(name))

        x_sb = sb("x_sb", [P, NJ, F])
        h_sb = sb("h_sb", [P, NJ, F])
        lin_sb = sb("lin_sb", [P, NJ, F])
        work = sb("work", [P, NG * GRP * TW])
        stat = sb("stat", [P, 3, NJ])
        rcount = sb("rcount", [P, NJ])
        hT = sb("hT", [P, 2, NP])
        agg_t = sb("agg_t", [P, NPAD])
        agg_m = sb("agg_m", [P, NPAD])
        dst_all = agg_t[:, 0:3 * CHUNK].bitcast(i32).rearrange("p (q e) -> p q e", q=3)
        low = sb("low", [P, 3])
        span = sb("span", [P, 3])
        base0 = sb("base0", [P, S])
        base = sb("base", [P, S])
        base_at = sb("base_at", [1, S], i32)
        span_row = sb("span_row", [1, 3 * P])
        over = sb("over", [1, NWIN])
        widest = sb("widest", [1, 2])
        npass = sb("npass", [1, 1], i32)
        src_sb = sb("src_sb", [P, 2, C], i32)
        dst_sb = sb("dst_sb", [P, 2, C], i32)
        sh_sb = sb("sh_sb", [P, 2, C, 4])
        rad_sb = sb("rad_sb", [P, 2, C * NB])
        local = sb("local", [P, C])
        onehot = sb("onehot", [P, 2, C, W])
        rows = sb("rows", [P, 2, C, 2 * F])
        radT = sb("radT", [C * NB, P])
        act1 = sb("act1", [P, 2, 3, P])
        act2 = sb("act2", [P, 2, PAIRS, P])
        coef = sb("coef", [P, 2, C, 3, MUL])
        coef_v = sb("coef_v", [P, 2, C, 3, MUL])
        dots = sb("dots", [P, C, MUL, 3])
        prod = work[:].rearrange("p (a t k) -> p a t k", a=NG, t=GRP)
        k_sb = sb("k_sb", [P, K_ALL])
        ident = k_sb[:, K_ID:K_ID + P]
        w_self0 = sb("w_self0", [P, P])
        w_self1 = sb("w_self1", [P, P])
        w_mean = sb("w_mean", [P, F + 1])
        bias0 = sb("bias0", [P, F])
        w1_sb = sb("w1_sb", [C * NB, PAIRS, P])
        w2_sb = sb("w2_sb", [P, P])
        lin_flat = lin_sb[:].rearrange("p j f -> p (j f)")
        w3_raw = lin_flat[:, 0:NTP]
        w3_sb = sb("w3_sb", [P, 2 * NTP])
        b1_sb = sb("b1_sb", [P, 1])
        b2_sb = sb("b2_sb", [P, 1])
        b3_raw = lin_flat[:, NTP:2 * NTP]
        b3_rest = lin_flat[:, 2 * NTP:5 * NTP].rearrange("p (a k) -> p a k", a=3)
        b3_part = sb("b3_part", [P, NTP], bf16)
        b3_sb = sb("b3_sb", [P, 2, NTP], bf16)
        pick3 = sb("pick3", [P, P], bf16)

        ps = ctx.enter_context(nc.psum_tensor("ps", [P, 8, 512], f32))
        PS_IN, PS_H = 6, 7
        PS_M, PS_T = 6, 7

        h_dram = [nc.dram_tensor(f"h{k}_dram", [N, F], f32, kind="Internal").ap() for k in range(2)]
        act2_dram = nc.dram_tensor("act2_dram", [S, P, PAIRS * P], f32, kind="Internal").ap()
        low_dram = nc.dram_tensor("low_dram", [3 * P], f32, kind="Internal").ap()
        span_dram = nc.dram_tensor("span_dram", [3 * P], f32, kind="Internal").ap()

        zeroed, zeroed2 = sem("zeroed"), sem("zeroed2")
        x_in, k_in, weights_in, dst_in = sem("x_in"), sem("k_in"), sem("weights_in"), sem("dst_in")
        bias_parts, prep = sem("bias_parts"), sem("prep")
        spans, spans_out, spans_in = sem("spans"), sem("spans_out"), sem("spans_in")
        tables = sem("tables")
        norm, squared, rooted = sem("norm"), sem("squared"), sem("rooted")
        h_ready, h_out = sem("h_ready"), sem("h_out")
        turned, hT_ready, self_ready, self_used = sem("turned"), sem("hT_ready"), sem("self_ready"), sem("self_used")
        summed, node_step, out_ready, out_sent = sem("summed"), sem("node_step"), sem("out_ready"), sem("out_sent")
        pool_go = sem("pool_go")

        class Layer:
            def __init__(self, k):
                self.start = sem(f"start{k}")
                self.src_in = [sem(f"src_in{k}{a}") for a in range(2)]
                self.dst_in = [sem(f"dst_in{k}{a}") for a in range(2)]
                self.rad_in = [sem(f"rad_in{k}{a}") for a in range(2)]
                self.rows_in = [sem(f"rows_in{k}{a}") for a in range(2)]
                self.based = sem(f"based{k}")
                self.masked = sem(f"masked{k}")
                self.onehot = sem(f"onehot{k}")
                self.scattered = sem(f"scattered{k}")
                self.added = sem(f"added{k}")
                self.tick = sem(f"tick{k}")
                self.shifted = sem(f"shifted{k}")

        L0, L1 = Layer(0), Layer(1)
        turned_in, radT_done = sem("turned_in"), sem("radT_done")
        hid1, act1_done, hid2, act2_done = sem("hid1"), sem("act1_done"), sem("hid2"), sem("act2_done")
        scaled, dotted, coef_done = sem("scaled"), sem("dotted"), sem("coef_done")
        act2_out = [sem(f"act2_out{a}") for a in range(2)]
        act2_in = [sem(f"act2_in{a}") for a in range(2)]
        tpw, prod_a, prod_b, reduced, feats = sem("tpw"), sem("prod_a"), sem("prod_b"), sem("reduced"), sem("feats")

        block = ctx.enter_context(nc.Block())

        NW = 4 + 1 + 1 + 4 + 12 + 12 + 2 + 2 + 2 + 2 + 1

        def hidden_of(s):
            return act2_dram[s] if isinstance(s, int) else act2_dram[bass.ds(s, 1)].rearrange("a p k -> p (a k)")

        @block.sync
        def _(sp):
            sp.dma_start(x_sb[0:NP], x.rearrange("(p j) f -> p j f", j=NJ)).then_inc(x_in, 16)
            sp.dma_start(k_sb[:], consts).then_inc(k_in, 16)
            sp.wait_ge(zeroed2, 1)
            full = 2 * P
            sp.dma_start(dst_all[:, 0:2], dst[0:full * CHUNK].rearrange("(q p e) -> p q e", q=2, e=CHUNK)).then_inc(dst_in, 16)
            sp.dma_start(dst_all[0:S - 1 - full, 2], dst[full * CHUNK:(S - 1) * CHUNK].rearrange("(p e) -> p e", e=CHUNK)).then_inc(dst_in, 16)
            sp.dma_start(dst_all[S - 1 - full:S - full, 2], dst[E - CHUNK:E].rearrange("(p e) -> p e", e=CHUNK)).then_inc(dst_in, 16)
            sp.wait_ge(zeroed, 1)
            for q in range(QB):
                sp.dma_start(w_self0[q * F:q * F + F, q * F:q * F + F], w0[0:F]).then_inc(weights_in, 16)
                sp.dma_start(w_self1[q * F:q * F + MUL, q * F:q * F + MUL], ws).then_inc(weights_in, 16)
                for i in range(3):
                    at = q * F + MUL + i
                    sp.dma_start(w_self1[at:at + 3 * MUL - 2:3, at:at + 3 * MUL - 2:3], wv).then_inc(weights_in, 16)
            sp.dma_start(w_mean[64:64 + F, 0:F], w0[F:2 * F]).then_inc(weights_in, 16)
            sp.dma_start(bias0[:], b0.unsqueeze(0).broadcast_to([P, F])).then_inc(weights_in, 16)
            for c in range(C):
                sp.dma_start(w1_sb[c * NB:c * NB + NB, c // 2, (c % 2) * HR:(c % 2) * HR + HR], w1).then_inc(weights_in, 16)
            for a in range(2):
                half = slice(a * HR, a * HR + HR)
                sp.dma_start(w2_sb[half, half], w2).then_inc(weights_in, 16)
                sp.dma_start(w3_raw[half], w3).then_inc(weights_in, 16)
                sp.dma_start(b1_sb[half], b1.unsqueeze(1)).then_inc(weights_in, 16)
                sp.dma_start(b2_sb[half], b2.unsqueeze(1)).then_inc(weights_in, 16)
            sp.dma_start(b3_raw, b3.unsqueeze(0).broadcast_to([P, NTP])).then_inc(weights_in, 16)
            sp.wait_ge(spans, 3)
            sp.dma_start(low_dram.rearrange("(q p) -> p q", q=3), low[:]).then_inc(spans_out, 16)
            sp.dma_start(span_dram.rearrange("(q p) -> p q", q=3), span[:]).then_inc(spans_out, 16)
            sp.wait_ge(spans_out, 32)
            sp.dma_start(base0[:], low_dram[0:S].unsqueeze(0).broadcast_to([P, S])).then_inc(spans_in, 16)
            sp.dma_start(span_row[:], span_dram.unsqueeze(0)).then_inc(spans_in, 16)
            sp.wait_ge(h_ready, 1)
            sp.dma_start(h_dram[0].rearrange("(p j) f -> p j f", j=NJ), h_sb[0:NP]).then_inc(h_out, 16)
            sp.wait_ge(tables, 1)
            passes = sp.value_load(npass[0:1, 0:1], min_val=1, max_val=NWIN)

            def load0(r, n, s, slot, use, then):
                sp.wait_ge(L0.added, n + 1)
                sp.dma_start(src_sb[:, slot], edges_of(s, src)).then_inc(L0.src_in[slot], 16)
                sp.dma_start(dst_sb[:, slot], edges_of(s, dst)).then_inc(L0.dst_in[slot], 16)
                sp.dma_start(rad_sb[:, slot], edges_of(s, ea8)).then_inc(L0.rad_in[slot], 16)
            walk(sp, passes, load0, lambda r: sp.wait_ge(L0.start, r + 1))

            sp.wait_ge(h_ready, 2)
            sp.dma_start(h_dram[1].rearrange("(p j) f -> p j f", j=NJ), h_sb[0:NP]).then_inc(h_out, 16)

            sp.wait_ge(act2_out[0], passes * (16 * ((S + 1) // 2)) + 16)
            sp.sem_inc(L1.tick)
            sp.wait_ge(act2_out[1], passes * (16 * (S // 2)) + 16)
            sp.sem_inc(L1.tick)

            def load1(r, n, s, slot, use, then):
                sp.wait_ge(scaled, n + 1)
                sp.dma_start(src_sb[:, slot], edges_of(s, src)).then_inc(L1.src_in[slot], 16)
                sp.wait_ge(tpw, n * NG + NG)
                sp.dma_start(act2[:, slot].rearrange("p q e -> p (q e)"), hidden_of(s)).then_inc(act2_in[slot], 16)
                sp.wait_ge(feats, n * NG + NG)
                sp.dma_start(dst_sb[:, slot], edges_of(s, dst)).then_inc(L1.dst_in[slot], 16)
                sp.dma_start(sh_sb[:, slot].rearrange("p c k -> p (c k)"), edges_of(s, ea4)).then_inc(L1.dst_in[slot], 16)
            walk(sp, passes, load1, lambda r: sp.wait_ge(L1.start, r + 1))

            for half in range(2):
                sp.wait_ge(out_ready, half + 1)
                js = slice(half * (NJ // 2), (half + 1) * (NJ // 2))
                sp.dma_start(out.rearrange("(p j) f -> p j f", j=NJ)[:, js], x_sb[0:NP, js]).then_inc(out_sent, 16)
            sp.wait_ge(out_sent, 32)

        @block.gpsimd
        def _(pool):
            pool.wait_ge(tables, 1)
            passes = pool.value_load(npass[0:1, 0:1], min_val=1, max_val=NWIN)
            for k, L in enumerate((L0, L1)):
                pool.wait_ge(h_out, 16 * (k + 1))
                pool.sem_inc(pool_go)

                def gather(r, n, s, slot, use, then):
                    pool.wait_ge(L.src_in[slot], use * 16 + 16)
                    pool.sem_inc(L.tick)
                    if k == 0:
                        pool.wait_ge(L.scattered, n + 1)
                        pool.sem_inc(L.tick)
                    else:
                        pool.wait_ge(scaled, n + 1)
                        pool.sem_inc(L.tick)
                        pool.wait_ge(dotted, n + 1)
                        pool.sem_inc(L.tick)
                    for c in range(C):
                        pool.indirect_dma_start(
                            out=rows[:, slot, c, 0:F], out_offset=None, in_=h_dram[k],
                            in_offset=bass.IndirectOffsetOnAxis(ap=src_sb[:, slot, c:c + 1], axis=0),
                            bounds_check=N - 1, oob_is_err=False).then_inc(L.rows_in[slot], 16)

                def start(r):
                    pool.wait_ge(L.start, r + 1)
                    pool.sem_inc(L.tick)
                walk(pool, passes, gather, start)

        @block.scalar
        def _(act):
            def norm_help(k):
                act.wait_ge(norm, 7 * k + 3)
                nc.scalar.activation(work[0:NP, 0:NJ * F], h_sb[0:NP].rearrange("p j f -> p (j f)"), ACT.Square).then_inc(squared, 1)
                act.wait_ge(norm, 7 * k + 5)
                nc.scalar.activation(stat[0:NP, 2], stat[0:NP, 1], ACT.Sqrt).then_inc(rooted, 1)

            def self_help(k):
                for q in range(NQ):
                    act.wait_ge(turned, k * NQ + q + 1)
                    if q + k * NQ >= 2:
                        act.wait_ge(self_ready, k * NQ + q - 1)
                    nc.scalar.activation(hT[:, q % 2], ps[:, q % 2, 0:NP], ACT.Copy).then_inc(hT_ready, 1)

            norm_help(0)
            self_help(0)
            act.sem_inc(act2_done, 1)
            for a in range(2):
                act.sem_inc(act2_out[a], 16)
            act.wait_ge(tables, 1)
            passes = act.value_load(npass[0:1, 0:1], min_val=1, max_val=NWIN)

            def mlp(r, n, s, slot, use, then):
                act.wait_ge(turned_in, n + 1)
                nc.scalar.activation(radT[:], ps[0:C * NB, PS_IN, 384:512], ACT.Copy).then_inc(radT_done, 1)
                for half in range(2):
                    act.wait_ge(hid1, n * 2 + (half + 1))
                    nc.scalar.activation(act1[:, half].rearrange("p q e -> p (q e)"), ps[:, PS_IN, 0:384], ACT.Silu,
                                         bias=b1_sb[:, 0:1]).then_inc(act1_done, 1)
                    act.wait_ge(hid2, n * 2 + (half + 1))
                    if half == 0:
                        act.wait_ge(act2_out[slot], use * 16 + 16)
                    nc.scalar.activation(act2[:, slot, half * 3:half * 3 + 3].rearrange("p q e -> p (q e)"), ps[:, PS_H, 0:384],
                                         ACT.Silu, bias=b2_sb[:, 0:1]).then_inc(act2_done, 1)
                act.wait_ge(act2_done, n * 2 + 3)
                act.dma_start(hidden_of(s), act2[:, slot].rearrange("p q e -> p (q e)")).then_inc(act2_out[slot], 16)
            walk(act, passes, mlp, lambda r: act.wait_ge(L0.start, r + 1))

            norm_help(1)
            self_help(1)
            act.sem_inc(scaled, 2)

            def scale(r, n, s, slot, use, then):
                act.wait_ge(L1.rows_in[slot], use * (16 * C) + 16 * C)
                act.wait_ge(L1.dst_in[slot], use * 32 + 32)
                act.wait_ge(prod_b, n * NG + NG)
                nc.scalar.activation(coef[:, slot, :, 0], rows[:, slot, :, 0:MUL], ACT.Copy)
                for c in range(C):
                    nc.scalar.activation(coef[:, slot, c, 1], rows[:, slot, c, 0:MUL], ACT.Copy,
                                         scale=sh_sb[:, slot, c, 0:1])
                    last_scale = nc.scalar.activation(
                        coef_v[:, slot, c], rows[:, slot, c, MUL:F].rearrange("p (u i) -> p i u", i=3), ACT.Copy,
                        scale=sh_sb[:, slot, c, 0:1])
                last_scale.then_inc(scaled, 1)
            walk(act, passes, scale, lambda r: act.wait_ge(L1.start, r + 1))

        @block.vector
        def _(dve):
            nc.vector.memset(dst_all[:, 2], 0).then_inc(zeroed2, 1)
            for t in (w_self0, w_self1, w_mean, w1_sb, w2_sb):
                nc.vector.memset(t[:], 0.0)
            nc.vector.memset(b3_sb[:], 0.0)
            nc.vector.memset(pick3[:], 0.0)
            nc.vector.memset(w3_sb[:], 0.0)
            nc.vector.memset(rows[:], 0.0)
            nc.vector.memset(agg_m[:], 0.0).then_inc(zeroed, 1)
            dve.wait_ge(zeroed, 1)
            nc.vector.memset(rows[:, :, :, F:F + 1], 1.0)
            nc.vector.memset(w_mean[96:97, F:F + 1], 1.0)
            for a in range(3):
                last = nc.vector.memset(pick3[32 * a:32 * a + 1], 1.0)
            last.then_inc(zeroed, 1)
            dve.wait_ge(zeroed, 2)

            def layer_norm(k):
                xv, hv, n0 = x_sb[0:NP], h_sb[0:NP], 7 * k
                mean, var, root = (stat[0:NP, a] for a in range(3))
                nc.vector.tensor_reduce(mean, xv, AX.X, ALU.add).then_inc(norm, 1)
                dve.wait_ge(norm, n0 + 1)
                nc.vector.tensor_scalar(mean, mean, 1.0 / F, None, ALU.mult).then_inc(norm, 1)
                dve.wait_ge(norm, n0 + 2)
                nc.vector.tensor_tensor(hv, xv, mean.unsqueeze(2).broadcast_to([NP, NJ, F]), ALU.subtract).then_inc(norm, 1)
                dve.wait_ge(squared, k + 1)
                nc.vector.tensor_reduce(var, work[0:NP, 0:NJ * F].rearrange("p (j f) -> p j f", f=F), AX.X, ALU.add).then_inc(norm, 1)
                dve.wait_ge(norm, n0 + 4)
                nc.vector.tensor_scalar(var, var, 1.0 / F, EPS, ALU.mult, ALU.add).then_inc(norm, 1)
                dve.wait_ge(rooted, k + 1)
                nc.vector.reciprocal(mean, root).then_inc(norm, 1)
                dve.wait_ge(norm, n0 + 6)
                nc.vector.tensor_tensor(hv, hv, mean.unsqueeze(2).broadcast_to([NP, NJ, F]), ALU.mult).then_inc(norm, 1)
                dve.wait_ge(norm, n0 + 7)
                nc.vector.tensor_scalar(hv, hv, 0.0, None, ALU.max).then_inc(h_ready, 1)

            def own_part(k):
                for q in range(NQ):
                    dve.wait_ge(self_ready, k * NQ + q + 1)
                    js = slice(q * QB, q * QB + QB)
                    got = ps[0:NP, 2 + q % 2, 0:P].rearrange("p (j f) -> p j f", f=F)
                    add = bias0[0:NP].unsqueeze(1).broadcast_to([NP, QB, F]) if k == 0 else x_sb[0:NP, js]
                    nc.vector.tensor_tensor(lin_sb[0:NP, js], got, add, ALU.add).then_inc(self_used, 1)

            dve.wait_ge(x_in, 16)
            layer_norm(0)

            dve.wait_ge(dst_in, 48)
            nc.vector.tensor_reduce(low[:], dst_all, AX.X, ALU.min).then_inc(spans, 1)
            nc.vector.tensor_reduce(span[:], dst_all, AX.X, ALU.max).then_inc(spans, 1)
            dve.wait_ge(spans, 2)
            nc.vector.tensor_tensor(span[:], span[:], low[:], ALU.subtract).then_inc(spans, 1)
            dve.wait_ge(spans_in, 32)
            nc.vector.tensor_reduce(widest[:, 0:1], span_row[:], AX.X, ALU.max).then_inc(prep, 1)
            dve.wait_ge(prep, 1)
            dve.wait_ge(k_in, 16)
            nc.vector.tensor_scalar(over[:], k_sb[0:1, K_THR:K_THR + NWIN], widest[:, 0:1], None, ALU.is_le).then_inc(prep, 1)
            dve.wait_ge(prep, 2)
            nc.vector.tensor_reduce(widest[:, 1:2], over[:], AX.X, ALU.add).then_inc(prep, 1)
            dve.wait_ge(prep, 3)
            nc.vector.tensor_scalar(npass[:], widest[:, 1:2], 1.0, None, ALU.add).then_inc(prep, 1)
            nc.vector.tensor_copy(base_at[:], base0[0:1]).then_inc(prep, 1)
            nc.vector.tensor_copy(base[:], base0[:]).then_inc(prep, 1)
            dve.wait_ge(prep, 6)
            nc.vector.memset(agg_t[:], 0.0).then_inc(tables, 1)

            dve.wait_ge(weights_in, 16 * NW)
            nc.vector.tensor_scalar(w_self1[:], w_self1[:], MUL ** -0.5, None, ALU.mult).then_inc(prep, 1)
            order = (2, 0, 1, 3)
            for a in range(2):
                half = slice(a * HR, a * HR + HR)
                for g, own in enumerate(order):
                    nc.vector.tensor_copy(
                        w3_sb[half, a * NTP + g * B:a * NTP + (g + 1) * B].rearrange("p (w u) -> p w u", w=MUL),
                        w3_raw[half, own * B:(own + 1) * B].rearrange("p (u w) -> p w u", w=MUL)).then_inc(prep, 1)
            for g, own in enumerate(order):
                last = nc.vector.tensor_copy(b3_rest[:, 0, g * B:(g + 1) * B].rearrange("p (w u) -> p w u", w=MUL),
                                             b3_raw[:, own * B:(own + 1) * B].rearrange("p (u w) -> p w u", w=MUL))
            last.then_inc(bias_parts, 1)
            dve.wait_ge(bias_parts, 1)
            for a in range(3):
                nc.vector.tensor_copy(b3_part[:], b3_rest[:, a]).then_inc(bias_parts, 1)
                dve.wait_ge(bias_parts, 2 + 4 * a)
                row = slice(32 * a, 32 * a + 1)
                nc.vector.tensor_copy(b3_sb[row, 0], b3_part[row]).then_inc(bias_parts, 1)
                nc.vector.tensor_copy(b3_sb[row, 1], b3_part[row]).then_inc(bias_parts, 1)
                nc.vector.tensor_tensor(b3_rest[:, (a + 1) % 3], b3_rest[:, a], b3_part[:], ALU.subtract).then_inc(bias_parts, 1)
                dve.wait_ge(bias_parts, 5 + 4 * a)
            own_part(0)

            passes = dve.value_load(npass[0:1, 0:1], min_val=1, max_val=NWIN)
            iota = k_sb[:, K_IOTA:K_IOTA + W].unsqueeze(1).broadcast_to([P, C, W])

            def one_hot(L, r, n, s, slot, between=None):
                start = base[:, s:s + 1] if isinstance(s, int) else base[:, bass.ds(s, 1)]
                nc.vector.tensor_tensor(local[:], dst_sb[:, slot], start.broadcast_to([P, C]), ALU.subtract).then_inc(L.based, 1)
                if between is not None:
                    between()
                dve.wait_ge(L.based, n + 1)
                if is_last(s):
                    nc.vector.memset(local[0:MASKED], -1.0).then_inc(L.masked, 1)
                    dve.wait_ge(L.masked, r + 1)
                nc.vector.tensor_tensor(onehot[:, slot], iota, local[:].unsqueeze(2).broadcast_to([P, C, W]),
                                        ALU.is_equal).then_inc(L.onehot, 1)

            def window(s):
                at = base_at[0:1, s:s + 1] if isinstance(s, int) else base_at[0:1, bass.ds(s, 1)]
                return dve.value_load(at, min_val=0, max_val=N)

            def next_windows(L, each, credit):
                def at_end(r):
                    dve.wait_ge(L.added, (r + 1) * (S * each) + credit)
                    nc.vector.tensor_scalar(base[:], base[:], float(W), None, ALU.add).then_inc(L.shifted, 1)
                    dve.wait_ge(L.shifted, r * 2 + 1)
                    nc.vector.tensor_scalar(base_at[:], base[0:1], float(N), None, ALU.min).then_inc(L.shifted, 1)
                    dve.wait_ge(L.shifted, r * 2 + 2)
                    dve.sem_inc(L.start)
                return at_end

            dve.sem_inc(L0.added, 2)
            dve.sem_inc(L0.start)

            def sum_rows(r, n, s, slot, use, then):
                dve.wait_ge(L0.dst_in[slot], use * 16 + 16)
                dve.wait_ge(L0.scattered, n + 1)
                one_hot(L0, r, n, s, slot)
                at = window(s)
                dve.wait_ge(L0.scattered, n + 3)
                dve.wait_ge(L0.added, n + 2)
                cols = agg_m[64:128, bass.ds(at, W)]
                nc.vector.tensor_tensor(cols, cols, ps[64:128, slot, 0:W], ALU.add).then_inc(L0.added, 1)
            walk(dve, passes, sum_rows, lambda r: None, next_windows(L0, 1, 2))

            nb = -(-NJ // JB)
            for b in range(nb):
                js = slice(b * JB, min(NJ, b * JB + JB))
                wide = js.stop - js.start
                got = ps[0:NP, b, 0:wide * (F + 1)].rearrange("p (j f) -> p j f", f=F + 1)
                if b == 0:
                    dve.wait_ge(h_out, 16)
                    nc.vector.tensor_copy(base_at[:], base0[0:1])
                    nc.vector.tensor_copy(base[:], base0[:]).then_inc(prep, 1)
                dve.wait_ge(summed, b + 1)
                nc.vector.tensor_scalar(rcount[0:NP, js], got[:, :, F], 1.0, None, ALU.max).then_inc(node_step, 1)
                dve.wait_ge(node_step, 5 * b + 1)
                nc.vector.reciprocal(rcount[0:NP, js], rcount[0:NP, js]).then_inc(node_step, 1)
                dve.wait_ge(node_step, 5 * b + 2)
                h = h_sb[0:NP, js]
                nc.vector.tensor_tensor(h, got[:, :, 0:F], rcount[0:NP, js].unsqueeze(2).broadcast_to([NP, wide, F]),
                                        ALU.mult).then_inc(node_step, 1)
                dve.wait_ge(node_step, 5 * b + 3)
                nc.vector.tensor_tensor(h, h, lin_sb[0:NP, js], ALU.add).then_inc(node_step, 1)
                dve.wait_ge(node_step, 5 * b + 4)
                nc.vector.scalar_tensor_tensor(out=x_sb[0:NP, js], in0=h, scalar=0.0, in1=x_sb[0:NP, js],
                                               op0=ALU.max, op1=ALU.add).then_inc(node_step, 1)
            dve.wait_ge(node_step, 5 * nb)
            layer_norm(1)
            own_part(1)
            dve.wait_ge(prep, 16)

            nc.vector.memset(prod[:, :, :, 0:B], 0.0)
            nc.vector.memset(agg_m[64:128], 0.0)
            dve.sem_inc(feats, 2 * NG)
            dve.sem_inc(prod_b, 2 * NG)
            dve.sem_inc(dotted, 2)
            dve.sem_inc(L1.added, 1)
            dve.sem_inc(L1.start)

            def weights_of(g):
                return ps[:, 2 * g:2 * g + 2].rearrange("p b (t k) -> p (b t) k", k=NTP)

            def add_window(n_added, at):
                dve.wait_ge(L1.added, n_added * 2 + 1)
                for agg, bank in ((agg_t, PS_T), (agg_m, PS_M)):
                    cols = agg[:, bass.ds(at, W)]
                    nc.vector.tensor_tensor(cols, cols, ps[:, bank, 0:W], ALU.add).then_inc(L1.added, 1)

            def products(r, n, s, slot, use, then):
                before = None if is_first(s) else window(s - 1)
                here = window(s) if is_last(s) else None
                dve.wait_ge(L1.dst_in[slot], use * 32 + 32)

                def vectors_by_sh1():
                    dve.wait_ge(L1.rows_in[slot], use * (16 * C) + 16 * C)
                    nc.vector.tensor_tensor(
                        dots[:], rows[:, slot, :, MUL:F].rearrange("p c (u i) -> p c u i", i=3),
                        sh_sb[:, slot, :, 1:4].unsqueeze(2).broadcast_to([P, C, MUL, 3]), ALU.mult).then_inc(dotted, 1)
                one_hot(L1, r, n, s, slot, vectors_by_sh1)
                dve.wait_ge(dotted, n + 3)
                nc.vector.tensor_reduce(coef[:, slot, :, 2], dots[:], AX.X, ALU.add).then_inc(coef_done, 1)

                def times_scalars(g):
                    m, ts = n * NG + g, slice(g * GRP, g * GRP + GRP)
                    dve.wait_ge(tpw, m + 1 + 2 * NG)
                    dve.wait_ge(L1.scattered, m + 1)
                    if g == 0:
                        dve.wait_ge(coef_done, n + 1)
                        dve.wait_ge(scaled, n + 3)
                    nc.vector.tensor_tensor(
                        prod[:, g, :, 4 * B:7 * B].rearrange("p t (g w u) -> p t g w u", g=3, w=MUL),
                        weights_of(g)[:, :, 0:3 * B].rearrange("p t (g w u) -> p t g w u", g=3, w=MUL),
                        coef[:, slot, ts].unsqueeze(3).broadcast_to([P, GRP, 3, MUL, MUL]), ALU.mult).then_inc(prod_a, 1)

                def times_vectors(g):
                    ts = slice(g * GRP, g * GRP + GRP)
                    nc.vector.tensor_tensor(
                        prod[:, g, :, B:4 * B].rearrange("p t (i w u) -> p t i w u", i=3, w=MUL),
                        weights_of(g)[:, :, 3 * B:4 * B].rearrange("p t (w u) -> p t w u", w=MUL).unsqueeze(2).broadcast_to([P, GRP, 3, MUL, MUL]),
                        coef_v[:, slot, ts].unsqueeze(3).broadcast_to([P, GRP, 3, MUL, MUL]), ALU.mult).then_inc(prod_b, 1)

                def sum_over_u(g):
                    m = n * NG + g
                    dve.wait_ge(prod_a, m + 1)
                    dve.wait_ge(prod_b, m + 1 + 2 * NG)
                    nc.vector.tensor_reduce(
                        prod[:, g, :, 0:3 * MUL], prod[:, g, :, 2 * B:5 * B].rearrange("p t (k u) -> p t k u", u=MUL),
                        AX.X, ALU.add).then_inc(reduced, 1)

                def times_sh1(g):
                    ts = slice(g * GRP, g * GRP + GRP)
                    dve.wait_ge(reduced, n * NG + g + 1)
                    nc.vector.tensor_tensor(
                        prod[:, g, :, 3 * MUL:6 * MUL].rearrange("p t (i w) -> p t i w", i=3),
                        prod[:, g, :, 2 * MUL:3 * MUL].unsqueeze(2).broadcast_to([P, GRP, 3, MUL]),
                        sh_sb[:, slot, ts, 1:4].unsqueeze(3).broadcast_to([P, GRP, 3, MUL]), ALU.mult).then_inc(feats, 1)

                times_scalars(0)
                times_vectors(0)
                if not is_first(s):
                    dve.wait_ge(L1.scattered, n * NG + 3)
                    add_window(n - 1, before)
                for g in range(1, NG):
                    times_scalars(g)
                    sum_over_u(g - 1)
                    times_vectors(g)
                    times_sh1(g - 1)
                sum_over_u(NG - 1)
                times_sh1(NG - 1)
                if is_last(s):
                    dve.wait_ge(L1.scattered, n * NG + NG + 3)
                    add_window(n, here)
            walk(dve, passes, products, lambda r: None, next_windows(L1, 2, 1))

            nb = -(-NJ // JC)
            dve.wait_ge(self_used, 2 * NQ)
            for b in range(nb):
                js = slice(b * JC, min(NJ, b * JC + JC))
                wide = js.stop - js.start
                dve.wait_ge(summed, -(-NJ // JB) + b + 1)
                ins = nc.vector.tensor_tensor(x_sb[0:NP, js], ps[0:NP, b, 0:wide * F].rearrange("p (j f) -> p j f", f=F),
                                              lin_sb[0:NP, js], ALU.add)
                if b in (3, nb - 1):
                    ins.then_inc(out_ready, 1)

        @block.tensor
        def _(pe):
            pe.wait_ge(k_in, 16)
            pe.wait_ge(weights_in, 16 * NW)
            pe.wait_ge(zeroed, 2)

            def own_part(k):
                wt = w_self0 if k == 0 else w_self1

                def product(q):
                    pe.wait_ge(hT_ready, k * NQ + q + 1)
                    if k * NQ + q >= 2:
                        pe.wait_ge(self_used, k * NQ + q - 1)
                    nc.tensor.matmul(ps[0:NP, 2 + q % 2, 0:P], hT[:, q % 2], wt[:], start=True, stop=True).then_inc(self_ready, 1)

                pe.wait_ge(h_ready, k + 1)
                for q in range(NQ):
                    if q >= 2:
                        pe.wait_ge(hT_ready, k * NQ + q - 1)
                    nc.tensor.transpose(ps[:, q % 2, 0:NP], h_sb[0:NP, q * QB:q * QB + QB].rearrange("p j f -> p (j f)"),
                                        k_sb[0:NP, K_ID:K_ID + NP]).then_inc(turned, 1)
                    if q >= 1:
                        product(q - 1)
                product(NQ - 1)

            own_part(0)
            pe.sem_inc(L0.scattered, 2)
            pe.wait_ge(tables, 1)
            passes = pe.value_load(npass[0:1, 0:1], min_val=1, max_val=NWIN)
            pe.wait_ge(self_used, NQ)

            def turn_in(n, slot, use):
                pe.wait_ge(L0.rad_in[slot], use * 16 + 16)
                nc.tensor.transpose(ps[0:C * NB, PS_IN, 384:512], rad_sb[:, slot], ident).then_inc(turned_in, 1)

            def hidden1(n, half):
                if half == 0:
                    pe.wait_ge(radT_done, n + 1)
                else:
                    pe.wait_ge(act1_done, n * 2 + 1)
                for q in range(3):
                    ins = nc.tensor.matmul(ps[:, PS_IN, q * P:q * P + P], w1_sb[:, half * 3 + q], radT[:], start=True, stop=True)
                ins.then_inc(hid1, 1)

            def hidden2(n, half):
                pe.wait_ge(act1_done, n * 2 + half + 1)
                pe.wait_ge(act2_done, n * 2 + half + 1)
                nc.tensor.matmul(ps[:, PS_H, 0:3 * P], w2_sb[:], act1[:, half].rearrange("p q e -> p (q e)"),
                                 start=True, stop=True).then_inc(hid2, 1)

            def sum_rows(r, n, s, slot, use, then):
                turn_in(n, slot, use)
                for half in range(2):
                    hidden1(n, half)
                    hidden2(n, half)
                pe.wait_ge(L0.rows_in[slot], use * (16 * C) + 16 * C)
                pe.wait_ge(L0.onehot, n + 1)
                pe.wait_ge(L0.added, n + 1)
                for c in range(C):
                    ins = nc.tensor.matmul(ps[64:128, slot, 0:W], rows[:, slot, c], onehot[:, slot, c],
                                           start=(c == 0), stop=(c == C - 1))
                ins.then_inc(L0.scattered, 1)
            walk(pe, passes, sum_rows, lambda r: pe.wait_ge(L0.start, r + 1))

            pe.wait_ge(L0.start, passes + 1)
            for b in range(-(-NJ // JB)):
                for j in range(b * JB, min(NJ, b * JB + JB)):
                    at = (j - b * JB) * (F + 1)
                    ins = nc.tensor.matmul(ps[0:NP, b, at:at + F + 1], agg_m[64:128, j:j + NJ * (NP - 1) + 1:NJ],
                                           w_mean[64:128], start=True, stop=True)
                ins.then_inc(summed, 1)
            pe.wait_ge(prep, 15)
            own_part(1)
            pe.wait_ge(self_used, 2 * NQ)
            pe.sem_inc(L1.scattered, 3)
            pe.sem_inc(tpw, 2 * NG)
            pe.wait_ge(bias_parts, 13)

            def weights(n, g, slot, use):
                if g == 0:
                    pe.wait_ge(act2_in[slot], use * 16 + 16)
                pe.wait_ge(prod_b, n * NG + (NG + 1 + g))
                for b in range(2):
                    bank = ps[:, 2 * g + b]
                    nc.tensor.matmul(bank, pick3[:], b3_sb[:].rearrange("p a k -> p (a k)"), start=True, stop=False)
                    ins = nc.tensor.matmul(bank, act2[:, slot, 2 * g + b], w3_sb[:], start=False, stop=True)
                ins.then_inc(tpw, 1)

            def scatter(n, g, slot):
                if g == 0:
                    pe.wait_ge(L1.onehot, n + 1)
                    pe.wait_ge(L1.added, n * 2 + 1)
                pe.wait_ge(feats, n * NG + g + 1 + 2 * NG)
                for t in range(GRP):
                    c = g * GRP + t
                    flags = dict(start=(c == 0), stop=(c == C - 1))
                    nc.tensor.matmul(ps[:, PS_T, 0:W], prod[:, g, t, 5 * B:7 * B], onehot[:, slot, c], **flags)
                    ins = nc.tensor.matmul(ps[:, PS_M, 0:W], prod[:, g, t, 0:2 * B], onehot[:, slot, c], **flags)
                ins.then_inc(L1.scattered, 1)

            def start(r):
                pe.wait_ge(L1.start, r + 1)
                weights(r * S, 0, 0, r * ((S + 1) // 2))
                weights(r * S, 1, 0, None)

            def group_steps(r, n, s, slot, use, then):
                weights(n, 2, slot, None)
                scatter(n, 0, slot)
                for g in range(2):
                    if not is_last(s):
                        weights(n + 1, g, 1 - slot, then)
                    scatter(n, g + 1, slot)
            walk(pe, passes, group_steps, start)

            pe.wait_ge(L1.start, passes + 1)
            for b in range(-(-NJ // JC)):
                for j in range(b * JC, min(NJ, b * JC + JC)):
                    at = (j - b * JC) * F
                    cols = slice(j, j + NJ * (NP - 1) + 1, NJ)
                    nc.tensor.matmul(ps[0:NP, b, at:at + F], agg_t[:, cols], k_sb[:, K_COMB:K_COMB + F], start=True, stop=False)
                    ins = nc.tensor.matmul(ps[0:NP, b, at:at + F], agg_m[:, cols], k_sb[:, K_COMB + F:K_COMB + 2 * F],
                                           start=False, stop=True)
                ins.then_inc(summed, 1)


_INS = ['x', 'src', 'dst', 'edge_attr_4', 'edge_attr_8', 'L0_gnn_W', 'L0_gnn_b', 'L1_gnn_W1', 'L1_gnn_b1', 'L1_gnn_W2',
        'L1_gnn_b2', 'L1_gnn_W3', 'L1_gnn_b3', 'L1_gnn_Ws', 'L1_gnn_Wv']


def kernel(**inputs):
    import numpy as np
    import concourse.bacc as bacc
    from concourse.bass_utils import run_bass_kernel_spmd

    nc = bacc.Bacc("TRN2", target_bir_lowering=False, num_devices=1)
    arrays, args = {}, []
    for name in _INS:
        arrays[f"in_{name}"] = np.ascontiguousarray(inputs[name])
    arrays["in_constants"] = constants()
    for name, a in arrays.items():
        args.append(nc.dram_tensor(name, a.shape, mybir.dt.from_np(a.dtype), kind="ExternalInput").ap())
    args.append(nc.dram_tensor("out_x", (N, F), mybir.dt.float32, kind="ExternalOutput").ap())
    gnn(nc, *args)
    result = run_bass_kernel_spmd(nc, [arrays], core_ids=[0])
    return result.results[0]["out_x"]
```

```python
import concourse.bass as bass
from concourse import mybir
from contextlib import ExitStack

N = 12500
E = 412500
F = 32
MUL = 8
HR = 64
NB = 8
NTP = 4 * MUL * MUL
EPS = 1e-5

P = 128
C = 12
CHUNK = P * C
S = -(-E // CHUNK)
TWICE = S * CHUNK - E
MASKED = TWICE // C
assert TWICE % C == 0 and S % 2 == 1
PAIRS = C // 2
W = 56
NWIN = -(-N // W)
NPAD = N + W
GRP = 4
NG = C // GRP
B = MUL * MUL
TW = 7 * B

NP = 125
NJ = N // NP
QB = P // F
NQ = NJ // QB
QN = N // QB
JB = 15
JC = 4


def cut(n, *wide):
    blocks, at = [], 0
    while at < n:
        step = wide[min(len(blocks), len(wide) - 1)]
        blocks.append(slice(at, min(n, at + step)))
        at += step
    return blocks


NORM_BLOCKS = [cut(NJ, NJ // 2), cut(NJ, JB, JB, JB, JB, JB, 12, 8, 5)]
assert len(NORM_BLOCKS[1]) <= 8
BLOCKS_BEFORE = [0, len(NORM_BLOCKS[0]), len(NORM_BLOCKS[0]) + len(NORM_BLOCKS[1])]
H_BLOCKS = [[1 + sum(js.stop < (q + 1) * NQ for js in blocks) for q in range(QB)] for blocks in NORM_BLOCKS]
SUM_BLOCKS = cut(NQ, JC)
OUT_PIECES = [(4, slice(0, 4 * JC)), (6, slice(4 * JC, 6 * JC)), (7, slice(6 * JC, NQ))]
assert len(SUM_BLOCKS) == OUT_PIECES[-1][0]

K_ID, K_IOTA, K_COMB, K_THR = 0, P, P + W, P + W + 2 * F
K_ALL = K_THR + NWIN


def constants():
    import numpy as np
    k = np.zeros((P, K_ALL), np.float32)
    k[:, K_ID:K_ID + P] = np.eye(P)
    k[:, K_IOTA:K_IOTA + W] = np.arange(W)
    scale = 1.0 / np.sqrt(2.0 * MUL) / np.sqrt(16.0)
    for w in range(MUL):
        for i in range(3):
            col = K_COMB + F + MUL + w * 3 + i
            if i > 0:
                k[(i - 1) * MUL + w, col] = scale
            k[(3 + i) * MUL + w, col] = scale
        for u in range(MUL):
            k[w * MUL + u, K_COMB + w] = scale
            k[B + w * MUL + u, K_COMB + w] = scale / np.sqrt(3.0)
            k[B + w * MUL + u, K_COMB + F + MUL + w * 3] = scale
    k[:, K_THR:] = np.arange(1, NWIN + 1) * W
    return k


def walk(eng, passes, step, at_start=None, at_end=None):
    even, odd = (S + 1) // 2, S // 2
    with eng.Fori(0, passes) as r:
        if at_start is not None:
            at_start(r)
        step(r=r, n=r * S, s=0, slot=0, use=r * even, then=r * odd)
        step(r=r, n=r * S + 1, s=1, slot=1, use=r * odd, then=r * even + 1)
        with eng.Fori(0, (S - 3) // 2) as i:
            step(r=r, n=r * S + i * 2 + 2, s=i * 2 + 2, slot=0, use=r * even + i + 1, then=r * odd + i + 1)
            step(r=r, n=r * S + i * 2 + 3, s=i * 2 + 3, slot=1, use=r * odd + i + 1, then=r * even + i + 2)
        step(r=r, n=r * S + (S - 1), s=S - 1, slot=0, use=r * even + (even - 1), then=None)
        if at_end is not None:
            at_end(r)


def is_early(s):
    return isinstance(s, int) and s < 2


def is_last(s):
    return isinstance(s, int) and s == S - 1


def edges_of(s, a):
    if isinstance(s, int):
        rows = a[min(s * CHUNK, E - CHUNK):min(s * CHUNK, E - CHUNK) + CHUNK]
    else:
        rows = a[bass.ds(s * CHUNK, CHUNK)]
    if len(rows.shape) == 1:
        return rows.rearrange("(p c) -> p c", c=C)
    return rows.rearrange("(p c) k -> p (c k)", c=C)


def gnn(nc, x, src, dst, ea4, ea8, w0, b0, w1, b1, w2, b2, w3, b3, ws, wv, consts, out):
    f32, i32 = mybir.dt.float32, mybir.dt.int32
    ALU, ACT, AX = mybir.AluOpType, mybir.ActivationFunctionType, mybir.AxisListType

    with ExitStack() as ctx:
        ctx.enter_context(nc.allow_non_contiguous_dma(reason="the small weights and tables, once"))

        def sb(name, shape, dt=f32):
            return ctx.enter_context(nc.sbuf_tensor(name, shape, dt))

        def sem(name):
            return ctx.enter_context(nc.semaphore(name))

        x_sb = sb("x_sb", [P, NJ, F])
        h_sb = sb("h_sb", [P, NJ, F])
        lin_sb = sb("lin_sb", [P, NJ, F])
        stat = sb("stat", [P, 3, NJ])
        eps_sb = sb("eps_sb", [P, 1])
        wide_sb = sb("wide_sb", [P, NJ * F])
        dst_two = wide_sb[:, 0:2 * CHUNK].bitcast(i32).rearrange("p (q e) -> p q e", q=2)
        squares = wide_sb[:].rearrange("p (j f) -> p j f", f=F)
        dst_rest = sb("dst_rest", [P, CHUNK], i32)
        rcount = sb("rcount", [P, NJ])
        hT = sb("hT", [P, 2, NP])
        agg = sb("agg", [P, NPAD])
        agg0 = agg[64:128]
        agg1 = agg[0:F]
        low = sb("low", [P, 3])
        span = sb("span", [P, 3])
        base0 = sb("base0", [P, S])
        base = sb("base", [P, S])
        base_at = sb("base_at", [1, S], i32)
        span_row = sb("span_row", [1, 3 * P])
        over = sb("over", [1, NWIN])
        widest = sb("widest", [1, 2])
        npass = sb("npass", [1, 1], i32)
        src_sb = sb("src_sb", [P, 2, C], i32)
        dst_sb = sb("dst_sb", [P, 2, C], i32)
        sh_sb = sb("sh_sb", [P, 2, C, 4])
        rad_sb = sb("rad_sb", [P, 2, C * NB])
        local = sb("local", [P, C])
        onehot = sb("onehot", [P, 2, C, W])
        rows = sb("rows", [P, 2, C, 2 * F])
        shared = sb("shared", [P, 2 * C * 2 * 3 * MUL + C * 3 * MUL])
        act1 = shared[:, 0:PAIRS * P].rearrange("p (a q e) -> p a q e", a=2, q=3)
        radT = shared[0:C * NB, PAIRS * P:PAIRS * P + P]
        n_coef = 2 * C * 3 * MUL
        coef = shared[:, 0:n_coef].rearrange("p (a c g u) -> p a c g u", a=2, c=C, g=3)
        coef_v = shared[:, n_coef:2 * n_coef].rearrange("p (a c i u) -> p a c i u", a=2, c=C, i=3)
        dots = shared[:, 2 * n_coef:].rearrange("p (c u i) -> p c u i", c=C, i=3)
        hidden = sb("hidden", [P, 2, C * P])
        act2 = hidden[:, :, 0:PAIRS * P]
        act2_1 = hidden
        prod = [sb(f"prod{a}", [P, C, TW]) for a in range(2)]
        quarters = prod[0][:].rearrange("p c k -> p (c k)")[:, 0:QN]
        k_sb = sb("k_sb", [P, K_ALL])
        ident = k_sb[:, K_ID:K_ID + P]
        w_self0 = sb("w_self0", [P, P])
        w_self1 = sb("w_self1", [P, P])
        w_mean = sb("w_mean", [P, F + 1])
        bias0 = sb("bias0", [P, F])
        w1_sb = sb("w1_sb", [C * NB, PAIRS, P])
        w2_sb = sb("w2_sb", [P, P])
        lin_flat = lin_sb[:].rearrange("p j f -> p (j f)")
        w3_raw = lin_flat[0:HR + 1, 0:NTP]
        w3_sb = sb("w3_sb", [P, NTP])
        sums_sb = sb("sums_sb", [P, 4 * B])
        turned_sb = sb("turned_sb", [P, 2, W])
        b1_sb = sb("b1_sb", [P, 1])
        b2_sb = sb("b2_sb", [P, 1])

        ps = ctx.enter_context(nc.psum_tensor("ps", [P, 8, 512], f32))
        PS_IN, PS_H = 6, 7
        PS_SUM, PS_TURN, COMB = 6, 7, 2 * P

        h_dram = [nc.dram_tensor(f"h{k}_dram", [N, F], f32, kind="Internal").ap() for k in range(2)]
        act2_dram = nc.dram_tensor("act2_dram", [S, HR, PAIRS, 2, P], f32, kind="Internal").ap()
        low_dram = nc.dram_tensor("low_dram", [3 * P], f32, kind="Internal").ap()
        span_dram = nc.dram_tensor("span_dram", [3 * P], f32, kind="Internal").ap()

        quartered, w1_in = sem("quartered"), sem("w1_in")
        zeroed, consts_set, agg_zeroed = sem("zeroed"), sem("consts_set"), sem("agg_zeroed")
        x_in, k_in, weights_in, dst_in = sem("x_in"), sem("k_in"), sem("weights_in"), sem("dst_in")
        prep, ones = sem("prep"), sem("ones")
        spans, spans_out, spans_in = sem("spans"), sem("spans_out"), sem("spans_in")
        tables = sem("tables")
        centred, squared, spread, rooted, inverted = (sem(t) for t in ("centred", "squared", "spread", "rooted", "inverted"))
        h_ready, h_out = sem("h_ready"), sem("h_out")
        turned, hT_ready, self_ready, self_used = sem("turned"), sem("hT_ready"), sem("self_ready"), sem("self_used")
        summed, node_step, out_ready, out_sent = sem("summed"), sem("node_step"), sem("out_ready"), sem("out_sent")

        class Layer:
            def __init__(self, k):
                self.opened = sem(f"opened{k}")
                self.src_in = [sem(f"src_in{k}{a}") for a in range(2)]
                self.dst_in = [sem(f"dst_in{k}{a}") for a in range(2)]
                self.rows_in = [[sem(f"rows_in{k}{a}{g}") for g in range(NG)] for a in range(2)]
                self.based = sem(f"based{k}")
                self.masked = sem(f"masked{k}")
                self.onehot = sem(f"onehot{k}")
                self.scattered = sem(f"scattered{k}")
                self.added = sem(f"added{k}")
                self.tick = sem(f"tick{k}")
                self.shifted = sem(f"shifted{k}")

        L0, L1 = Layer(0), Layer(1)
        rad_in = [sem(f"rad_in{a}") for a in range(2)]
        turned_in, radT_done = sem("turned_in"), sem("radT_done")
        hid1, act1_done, hid2, act2_done = sem("hid1"), sem("act1_done"), sem("hid2"), sem("act2_done")
        scaled, dotted, coef_done = sem("scaled"), sem("dotted"), sem("coef_done")
        act2_out = [sem(f"act2_out{a}") for a in range(2)]
        act2_in = [sem(f"act2_in{a}") for a in range(2)]
        copied, sums_turned = sem("copied"), sem("sums_turned")
        turned_copied, combined = sem("turned_copied"), sem("combined")
        tpw, prod_a, prod_b, reduced, feats = sem("tpw"), sem("prod_a"), sem("prod_b"), sem("reduced"), sem("feats")

        block = ctx.enter_context(nc.Block())

        NW = QB * 5 + 2 + 2 * 3 + 2
        full = 2 * P

        def by_quarters(t):
            return t.rearrange("p (q j) f -> p q j f", q=QB)

        def by_node(t):
            return t.rearrange("(q p j) f -> p q j f", q=QB, j=NQ)

        def nodes_of(j):
            first = (j // NQ) * QN + j % NQ
            return slice(first, first + NQ * (NP - 1) + 1, NQ)

        def hidden_of(s):
            at = act2_dram[s:s + 1] if isinstance(s, int) else act2_dram[bass.ds(s, 1)]
            return at.rearrange("a h q b e -> h (a q) b e")

        @block.sync
        def _(sp):
            sp.dma_start(dst_two, dst[0:full * CHUNK].rearrange("(q p e) -> p q e", q=2, e=CHUNK)).then_inc(dst_in, 16)
            sp.dma_start(dst_rest[0:S - 1 - full], dst[full * CHUNK:(S - 1) * CHUNK].rearrange("(p e) -> p e", e=CHUNK)).then_inc(dst_in, 16)
            sp.dma_start(dst_rest[S - 1 - full:S - full], dst[E - CHUNK:E].rearrange("(p e) -> p e", e=CHUNK)).then_inc(dst_in, 16)
            sp.dma_start(by_quarters(x_sb[0:NP]), by_node(x)).then_inc(x_in, 16)
            sp.dma_start(k_sb[:], consts).then_inc(k_in, 16)
            sp.wait_ge(zeroed, 1)
            for q in range(QB):
                sp.dma_start(w_self0[q * F:q * F + F, q * F:q * F + F], w0[0:F]).then_inc(weights_in, 16)
                sp.dma_start(w_self1[q * F:q * F + MUL, q * F:q * F + MUL], ws).then_inc(weights_in, 16)
                for i in range(3):
                    at = q * F + MUL + i
                    sp.dma_start(w_self1[at:at + 3 * MUL - 2:3, at:at + 3 * MUL - 2:3], wv).then_inc(weights_in, 16)
            sp.dma_start(w_mean[64:64 + F, 0:F], w0[F:2 * F]).then_inc(weights_in, 16)
            sp.dma_start(bias0[:], b0.unsqueeze(0).broadcast_to([P, F])).then_inc(weights_in, 16)

            def write_h(k):
                for q in range(QB):
                    sp.wait_ge(h_ready, BLOCKS_BEFORE[k] + H_BLOCKS[k][q])
                    sp.dma_start(by_node(h_dram[k])[:, q], by_quarters(h_sb[0:NP])[:, q]).then_inc(h_out, 16)

            sp.wait_ge(spans, 6)
            sp.dma_start(low_dram.rearrange("(q p) -> p q", q=3), low[:]).then_inc(spans_out, 16)
            sp.dma_start(span_dram.rearrange("(q p) -> p q", q=3), span[:]).then_inc(spans_out, 16)
            sp.wait_ge(spans_out, 32)
            sp.dma_start(base0[:], low_dram[0:S].unsqueeze(0).broadcast_to([P, S])).then_inc(spans_in, 16)
            sp.dma_start(span_row[:], span_dram.unsqueeze(0)).then_inc(spans_in, 16)
            write_h(0)
            sp.wait_ge(tables, 1)
            passes = sp.value_load(npass[0:1, 0:1], min_val=1, max_val=NWIN)

            def load0(r, n, s, slot, use, then):
                sp.wait_ge(L0.added, n + 1)
                sp.dma_start(src_sb[:, slot], edges_of(s, src)).then_inc(L0.src_in[slot], 16)
                sp.dma_start(dst_sb[:, slot], edges_of(s, dst)).then_inc(L0.dst_in[slot], 16)
                sp.dma_start(rad_sb[:, slot], edges_of(s, ea8)).then_inc(rad_in[slot], 16)
            walk(sp, passes, load0, lambda r: sp.wait_ge(L0.opened, r + 1))
            write_h(1)

            sp.wait_ge(act2_out[0], passes * (32 * ((S + 1) // 2)) + 32)
            sp.sem_inc(L1.tick)
            sp.wait_ge(act2_out[1], passes * (32 * (S // 2)) + 32)
            sp.sem_inc(L1.tick)

            def load1(r, n, s, slot, use, then):
                sp.wait_ge(scaled, n * NG + NG)
                sp.dma_start(src_sb[:, slot], edges_of(s, src)).then_inc(L1.src_in[slot], 16)
                sp.wait_ge(tpw, n * NG + NG)
                sp.dma_start(act2_1[0:HR, slot], hidden_of(s).rearrange("h q b e -> h (q b e)")).then_inc(act2_in[slot], 16)
                sp.wait_ge(feats, n * NG + NG)
                sp.dma_start(dst_sb[:, slot], edges_of(s, dst)).then_inc(L1.dst_in[slot], 16)
                sp.dma_start(sh_sb[:, slot].rearrange("p c k -> p (c k)"), edges_of(s, ea4)).then_inc(L1.dst_in[slot], 16)
            walk(sp, passes, load1, lambda r: sp.wait_ge(L1.opened, r + 1))

            for banks, js in OUT_PIECES:
                sp.wait_ge(out_ready, banks)
                sp.dma_start(by_node(out)[:, :, js], by_quarters(x_sb[0:NP])[:, :, js]).then_inc(out_sent, 16)
            sp.wait_ge(out_sent, 16 * len(OUT_PIECES))

        @block.gpsimd
        def _(pool):
            for t in (w_self0, w_self1, w_mean, w1_sb, w2_sb, w3_sb):
                nc.gpsimd.memset(t[:], 0.0)
            nc.gpsimd.memset(eps_sb[:], EPS)
            nc.gpsimd.memset(rows[:, :, :, F:2 * F], 0.0).then_inc(zeroed, 1)
            pool.wait_ge(zeroed, 1)
            nc.gpsimd.memset(w_mean[96:97, F:F + 1], 1.0).then_inc(zeroed, 1)
            pool.wait_ge(zeroed, 2)
            nc.gpsimd.memset(rows[:, :, :, F:F + 1], 1.0).then_inc(consts_set, 1)
            nc.gpsimd.memset(agg[:], 0.0).then_inc(agg_zeroed, 1)
            nc.gpsimd.memset(sums_sb[:], 0.0)
            for t in prod:
                nc.gpsimd.memset(t[:, :, 6 * MUL:B], 0.0).then_inc(consts_set, 1)
            for c in range(C):
                pool.dma_start(w1_sb[c * NB:c * NB + NB, c // 2, (c % 2) * HR:(c % 2) * HR + HR], w1).then_inc(w1_in, 16)
            pool.wait_ge(tables, 1)
            passes = pool.value_load(npass[0:1, 0:1], min_val=1, max_val=NWIN)
            for k, L in enumerate((L0, L1)):
                pool.wait_ge(h_out, 16 * QB * (k + 1))
                pool.sem_inc(L.tick)

                def gather(r, n, s, slot, use, then):
                    pool.wait_ge(L.src_in[slot], use * 16 + 16)
                    pool.sem_inc(L.tick)
                    if k == 0:
                        pool.wait_ge(L.scattered, n + 1)
                        pool.sem_inc(L.tick)
                    else:
                        pool.wait_ge(scaled, n * NG + NG)
                        pool.sem_inc(L.tick)
                        pool.wait_ge(dotted, n * NG + NG)
                        pool.sem_inc(L.tick)
                    for c in range(C):
                        pool.indirect_dma_start(
                            out=rows[:, slot, c, 0:F], out_offset=None, in_=h_dram[k],
                            in_offset=bass.IndirectOffsetOnAxis(ap=src_sb[:, slot, c:c + 1], axis=0),
                            bounds_check=N - 1, oob_is_err=False).then_inc(L.rows_in[slot][c // GRP], 16)

                def start(r):
                    pool.wait_ge(L.opened, r + 1)
                    pool.sem_inc(L.tick)
                walk(pool, passes, gather, start)

        @block.scalar
        def _(act):
            act.wait_ge(zeroed, 1)
            nc.scalar.activation(stat[:, 2, 0:1], eps_sb[:], ACT.Sqrt)
            for a in range(2):
                half = slice(a * HR, a * HR + HR)
                act.dma_start(w2_sb[half, half], w2).then_inc(weights_in, 16)
                act.dma_start(b1_sb[half], b1.unsqueeze(1)).then_inc(weights_in, 16)
                act.dma_start(b2_sb[half], b2.unsqueeze(1)).then_inc(weights_in, 16)
            act.dma_start(w3_raw[0:HR], w3).then_inc(weights_in, 16)
            act.dma_start(w3_raw[HR:HR + 1], b3.unsqueeze(0)).then_inc(weights_in, 16)

            def norm_help(k):
                for b, js in enumerate(NORM_BLOCKS[k]):
                    m = BLOCKS_BEFORE[k] + b
                    act.wait_ge(centred, 2 * m + 2)
                    nc.scalar.activation(squares[0:NP, js], h_sb[0:NP, js], ACT.Square).then_inc(squared, 1)
                    act.wait_ge(spread, m + 1)
                    nc.scalar.activation(stat[0:NP, 2, js], stat[0:NP, 1, js], ACT.Sqrt, bias=eps_sb[0:NP, 0:1],
                                         scale=1.0 / F).then_inc(rooted, 1)

            def self_help(k):
                for q in range(NQ):
                    act.wait_ge(turned, k * NQ + q + 1)
                    if q + k * NQ >= 2:
                        act.wait_ge(self_ready, k * NQ + q - 1)
                    nc.scalar.activation(hT[:, q % 2], ps[:, q % 2, 0:NP], ACT.Copy).then_inc(hT_ready, 1)

            norm_help(0)
            self_help(0)
            act.sem_inc(act2_done, 1)
            for a in range(2):
                act.sem_inc(act2_out[a], 32)
            act.sem_inc(scaled, 2 * NG)
            act.sem_inc(copied, 1)
            act.wait_ge(tables, 1)
            passes = act.value_load(npass[0:1, 0:1], min_val=1, max_val=NWIN)

            def mlp(r, n, s, slot, use, then):
                act.wait_ge(turned_in, n + 1)
                nc.scalar.activation(radT, ps[0:C * NB, PS_IN, 384:512], ACT.Copy).then_inc(radT_done, 1)
                for half in range(2):
                    act.wait_ge(hid1, n * 2 + (half + 1))
                    nc.scalar.activation(act1[:, half].rearrange("p q e -> p (q e)"), ps[:, PS_IN, 0:384], ACT.Silu,
                                         bias=b1_sb[:, 0:1]).then_inc(act1_done, 1)
                    act.wait_ge(hid2, n * 2 + (half + 1))
                    if half == 0:
                        act.wait_ge(act2_out[slot], use * 32 + 32)
                    nc.scalar.activation(act2[:, slot, half * 3 * P:(half + 1) * 3 * P], ps[:, PS_H, 0:384],
                                         ACT.Silu, bias=b2_sb[:, 0:1]).then_inc(act2_done, 1)
                act.wait_ge(act2_done, n * 2 + 3)
                for b in range(2):
                    act.dma_start(hidden_of(s)[:, :, b], act2[b * HR:(b + 1) * HR, slot].rearrange("h (q e) -> h q e", e=P)
                                  ).then_inc(act2_out[slot], 16)
            walk(act, passes, mlp, lambda r: act.wait_ge(L0.opened, r + 1))

            act.wait_ge(act2_out[0], passes * (32 * ((S + 1) // 2)) + 32)
            act.sem_inc(L1.tick)
            act.wait_ge(act2_out[1], passes * (32 * (S // 2)) + 32)
            act.sem_inc(L1.tick)
            zero, one = ident[HR:P, 0:1], ident[HR:HR + 1, HR:HR + 1]
            flat = hidden[:].rearrange("p a e -> p (a e)")
            nc.scalar.activation(flat[HR:P], zero.broadcast_to([P - HR, 2 * C * P]), ACT.Copy).then_inc(ones, 1)
            act.wait_ge(ones, 1)
            nc.scalar.activation(flat[HR:HR + 1], one.broadcast_to([1, 2 * C * P]), ACT.Copy).then_inc(ones, 1)

            norm_help(1)
            self_help(1)

            def copy_sums(n):
                act.wait_ge(L1.scattered, n * NG + 3 * NG)
                nc.scalar.activation(sums_sb[0:W], ps[0:W, PS_SUM, 0:4 * B], ACT.Copy).then_inc(copied, 1)

            def copy_turned(n):
                act.wait_ge(sums_turned, n + 1)
                act.wait_ge(combined, n + 1)
                nc.scalar.activation(turned_sb[:], ps[:, PS_TURN, 0:2 * P].rearrange("p (k e) -> p k e", k=2)[:, :, 0:W],
                                     ACT.Copy).then_inc(turned_copied, 1)

            def scale(r, n, s, slot, use, then):
                act.wait_ge(L1.dst_in[slot], use * 32 + 32)
                act.wait_ge(prod_b, n * NG + NG)
                for g in range(NG):
                    ts = slice(g * GRP, g * GRP + GRP)
                    act.wait_ge(L1.rows_in[slot][g], use * (16 * GRP) + 16 * GRP)
                    nc.scalar.activation(coef[:, slot, ts, 0], rows[:, slot, ts, 0:MUL], ACT.Copy)
                    for c in range(ts.start, ts.stop):
                        nc.scalar.activation(coef[:, slot, c, 1], rows[:, slot, c, 0:MUL], ACT.Copy,
                                             scale=sh_sb[:, slot, c, 0:1])
                        last_scale = nc.scalar.activation(
                            coef_v[:, slot, c], rows[:, slot, c, MUL:F].rearrange("p (u i) -> p i u", i=3), ACT.Copy,
                            scale=sh_sb[:, slot, c, 0:1])
                    last_scale.then_inc(scaled, 1)
                    if g == 0 and not is_early(s):
                        copy_sums(n - 2)
                        copy_turned(n - 2)
                if is_last(s):
                    copy_sums(n - 1)
                    copy_turned(n - 1)
                    copy_sums(n)
                    copy_turned(n)
            walk(act, passes, scale, lambda r: act.wait_ge(L1.opened, r + 1))

            act.wait_ge(L1.opened, passes + 1)
            nc.scalar.activation(quarters[(QB - 1) * F:], agg1[:, (QB - 1) * QN:N], ACT.Copy).then_inc(quartered, 1)

        @block.vector
        def _(dve):
            dve.sem_inc(L0.opened)
            dve.sem_inc(L1.opened)
            dve.sem_inc(L0.added, 2)
            dve.sem_inc(L1.added, 1)
            dve.sem_inc(feats, 2 * NG)
            dve.sem_inc(prod_b, 2 * NG)
            dve.sem_inc(dotted, 2 * NG)

            def centre(k, b):
                js, m = NORM_BLOCKS[k][b], BLOCKS_BEFORE[k] + b
                xv, hv, total = x_sb[0:NP, js], h_sb[0:NP, js], stat[0:NP, 0, js]
                nc.vector.tensor_reduce(total, xv, AX.X, ALU.add).then_inc(centred, 1)
                dve.wait_ge(centred, 2 * m + 1)
                nc.vector.scalar_tensor_tensor(out=hv, in0=total.unsqueeze(2).broadcast_to([NP, js.stop - js.start, F]),
                                               scalar=-1.0 / F, in1=xv, op0=ALU.mult, op1=ALU.add).then_inc(centred, 1)

            def sum_squares(k, b):
                js, m = NORM_BLOCKS[k][b], BLOCKS_BEFORE[k] + b
                dve.wait_ge(squared, m + 1)
                nc.vector.tensor_reduce(stat[0:NP, 1, js], squares[0:NP, js], AX.X, ALU.add).then_inc(spread, 1)

            def divide(k, b):
                js, m = NORM_BLOCKS[k][b], BLOCKS_BEFORE[k] + b
                hv, inverse = h_sb[0:NP, js], stat[0:NP, 0, js]
                dve.wait_ge(rooted, m + 1)
                nc.vector.reciprocal(inverse, stat[0:NP, 2, js]).then_inc(inverted, 1)
                dve.wait_ge(inverted, m + 1)
                nc.vector.scalar_tensor_tensor(out=hv, in0=hv, scalar=0.0, in1=inverse.unsqueeze(2).broadcast_to([NP, js.stop - js.start, F]),
                                               op0=ALU.max, op1=ALU.mult).then_inc(h_ready, 1)

            def own_part(k):
                for q in range(NQ):
                    dve.wait_ge(self_ready, k * NQ + q + 1)
                    js = slice(q * QB, q * QB + QB)
                    got = ps[0:NP, 2 + q % 2, 0:P].rearrange("p (j f) -> p j f", f=F)
                    add = bias0[0:NP].unsqueeze(1).broadcast_to([NP, QB, F]) if k == 0 else x_sb[0:NP, js]
                    nc.vector.tensor_tensor(lin_sb[0:NP, js], got, add, ALU.add).then_inc(self_used, 1)

            def reach(chunks, columns, edges):
                nc.vector.tensor_reduce(low[chunks, columns], edges, AX.X, ALU.min).then_inc(spans, 1)
                nc.vector.tensor_reduce(span[chunks, columns], edges, AX.X, ALU.max).then_inc(spans, 1)

            nc.vector.memset(low[:], 0.0)
            nc.vector.memset(span[:], 0.0).then_inc(spans, 1)
            dve.wait_ge(spans, 1)
            dve.wait_ge(dst_in, 48)
            reach(slice(0, P), slice(0, 2), dst_two)
            dve.wait_ge(x_in, 16)
            centre(0, 0)
            reach(slice(0, S - full), slice(2, 3), dst_rest[0:S - full].unsqueeze(1))
            dve.wait_ge(spans, 5)
            nc.vector.tensor_tensor(span[:], span[:], low[:], ALU.subtract).then_inc(spans, 1)
            centre(0, 1)
            for step in (sum_squares, divide):
                for b in range(len(NORM_BLOCKS[0])):
                    step(0, b)
            dve.wait_ge(spans_in, 32)
            nc.vector.tensor_reduce(widest[:, 0:1], span_row[:], AX.X, ALU.max).then_inc(prep, 1)
            dve.wait_ge(prep, 1)
            dve.wait_ge(k_in, 16)
            nc.vector.tensor_scalar(over[:], k_sb[0:1, K_THR:K_THR + NWIN], widest[:, 0:1], None, ALU.is_le).then_inc(prep, 1)
            dve.wait_ge(prep, 2)
            nc.vector.tensor_reduce(widest[:, 1:2], over[:], AX.X, ALU.add).then_inc(prep, 1)
            dve.wait_ge(prep, 3)
            nc.vector.tensor_scalar(npass[:], widest[:, 1:2], 1.0, None, ALU.add).then_inc(prep, 1)
            nc.vector.tensor_copy(base_at[:], base0[0:1]).then_inc(prep, 1)
            nc.vector.tensor_copy(base[:], base0[:]).then_inc(prep, 1)
            dve.wait_ge(prep, 6)
            dve.sem_inc(tables)

            dve.wait_ge(weights_in, 16 * NW)
            nc.vector.tensor_scalar(w_self1[:], w_self1[:], MUL ** -0.5, None, ALU.mult).then_inc(prep, 1)
            for g, own in enumerate((2, 0, 1, 3)):
                nc.vector.tensor_copy(w3_sb[0:HR + 1, g * B:(g + 1) * B].rearrange("p (w u) -> p w u", w=MUL),
                                      w3_raw[:, own * B:(own + 1) * B].rearrange("p (u w) -> p w u", w=MUL)).then_inc(prep, 1)
            dve.wait_ge(prep, 11)
            own_part(0)

            passes = dve.value_load(npass[0:1, 0:1], min_val=1, max_val=NWIN)
            iota = k_sb[:, K_IOTA:K_IOTA + W].unsqueeze(1).broadcast_to([P, C, W])

            def one_hot(L, r, n, s, slot):
                start = base[:, s:s + 1] if isinstance(s, int) else base[:, bass.ds(s, 1)]
                nc.vector.tensor_tensor(local[:], dst_sb[:, slot], start.broadcast_to([P, C]), ALU.subtract).then_inc(L.based, 1)
                dve.wait_ge(L.based, n + 1)
                if is_last(s):
                    nc.vector.memset(local[0:MASKED], -1.0).then_inc(L.masked, 1)
                    dve.wait_ge(L.masked, r + 1)
                nc.vector.tensor_tensor(onehot[:, slot], iota, local[:].unsqueeze(2).broadcast_to([P, C, W]),
                                        ALU.is_equal).then_inc(L.onehot, 1)

            def window(s):
                at = base_at[0:1, s:s + 1] if isinstance(s, int) else base_at[0:1, bass.ds(s, 1)]
                return dve.value_load(at, min_val=0, max_val=N)

            def next_windows(L, credit):
                def at_end(r):
                    dve.wait_ge(L.added, (r + 1) * S + credit)
                    dve.sem_inc(L.opened)
                    nc.vector.tensor_scalar(base[:], base[:], float(W), None, ALU.add).then_inc(L.shifted, 1)
                    dve.wait_ge(L.shifted, r * 2 + 1)
                    nc.vector.tensor_scalar(base_at[:], base[0:1], float(N), None, ALU.min).then_inc(L.shifted, 1)
                    dve.wait_ge(L.shifted, r * 2 + 2)
                return at_end

            dve.wait_ge(agg_zeroed, 1)

            def sum_rows(r, n, s, slot, use, then):
                dve.wait_ge(L0.dst_in[slot], use * 16 + 16)
                dve.wait_ge(L0.scattered, n + 1)
                one_hot(L0, r, n, s, slot)
                at = window(s)
                dve.wait_ge(L0.scattered, n + 3)
                dve.wait_ge(L0.added, n + 2)
                cols = agg0[:, bass.ds(at, W)]
                nc.vector.tensor_tensor(cols, cols, ps[64:128, slot, 0:W], ALU.add).then_inc(L0.added, 1)
            walk(dve, passes, sum_rows, at_end=next_windows(L0, 2))

            def add_mean(b):
                js = NORM_BLOCKS[1][b]
                wide = js.stop - js.start
                got = ps[0:NP, b, 0:wide * (F + 1)].rearrange("p (j f) -> p j f", f=F + 1)
                if b == 0:
                    dve.wait_ge(h_out, 16 * QB)
                    nc.vector.tensor_copy(base_at[:], base0[0:1])
                    nc.vector.tensor_copy(base[:], base0[:]).then_inc(prep, 1)
                dve.wait_ge(summed, b + 1)
                nc.vector.tensor_scalar(rcount[0:NP, js], got[:, :, F], 1.0, None, ALU.max).then_inc(node_step, 1)
                dve.wait_ge(node_step, 5 * b + 1)
                nc.vector.reciprocal(rcount[0:NP, js], rcount[0:NP, js]).then_inc(node_step, 1)
                dve.wait_ge(node_step, 5 * b + 2)
                h = h_sb[0:NP, js]
                nc.vector.tensor_tensor(h, got[:, :, 0:F], rcount[0:NP, js].unsqueeze(2).broadcast_to([NP, wide, F]),
                                        ALU.mult).then_inc(node_step, 1)
                dve.wait_ge(node_step, 5 * b + 3)
                nc.vector.tensor_tensor(h, h, lin_sb[0:NP, js], ALU.add).then_inc(node_step, 1)
                dve.wait_ge(node_step, 5 * b + 4)
                nc.vector.scalar_tensor_tensor(out=x_sb[0:NP, js], in0=h, scalar=0.0, in1=x_sb[0:NP, js],
                                               op0=ALU.max, op1=ALU.add).then_inc(node_step, 1)
                dve.wait_ge(node_step, 5 * b + 5)

            for b in range(len(NORM_BLOCKS[1])):
                add_mean(b)
                centre(1, b)
                if b > 0:
                    divide(1, b - 1)
                sum_squares(1, b)
            divide(1, b)
            own_part(1)
            dve.wait_ge(prep, 12)

            dve.wait_ge(consts_set, 3)

            def weights_of(g):
                return ps[:, 2 * g:2 * g + 2].rearrange("p b (t k) -> p (b t) k", k=NTP)

            def add_window(n_added, at):
                dve.wait_ge(combined, n_added + 2)
                dve.wait_ge(L1.added, n_added + 1)
                cols = agg1[:, bass.ds(at, W)]
                nc.vector.tensor_tensor(cols, cols, ps[0:F, PS_TURN, COMB:COMB + W], ALU.add).then_inc(L1.added, 1)

            def products(r, n, s, slot, use, then):
                before2 = None if is_early(s) else window(s - 2)
                dve.wait_ge(L1.dst_in[slot], use * 32 + 32)
                dve.wait_ge(L1.scattered, n * NG + NG)
                one_hot(L1, r, n, s, slot)

                def vectors_by_sh1(g):
                    ts = slice(g * GRP, g * GRP + GRP)
                    dve.wait_ge(L1.rows_in[slot][g], use * (16 * GRP) + 16 * GRP)
                    nc.vector.tensor_tensor(
                        dots[:, ts], rows[:, slot, ts, MUL:F].rearrange("p c (u i) -> p c u i", i=3),
                        sh_sb[:, slot, ts, 1:4].unsqueeze(2).broadcast_to([P, GRP, MUL, 3]), ALU.mult).then_inc(dotted, 1)

                def sum_over_i(g):
                    ts = slice(g * GRP, g * GRP + GRP)
                    dve.wait_ge(dotted, n * NG + g + 1 + 2 * NG)
                    nc.vector.tensor_reduce(coef[:, slot, ts, 2], dots[:, ts], AX.X, ALU.add).then_inc(coef_done, 1)

                def times_scalars(g):
                    m, ts = n * NG + g, slice(g * GRP, g * GRP + GRP)
                    dve.wait_ge(tpw, m + 1 + 2 * NG)
                    dve.wait_ge(coef_done, m + 1)
                    dve.wait_ge(scaled, m + 1 + 2 * NG)
                    nc.vector.tensor_tensor(
                        prod[slot][:, ts, 4 * B:7 * B].rearrange("p t (g w u) -> p t g w u", g=3, w=MUL),
                        weights_of(g)[:, :, 0:3 * B].rearrange("p t (g w u) -> p t g w u", g=3, w=MUL),
                        coef[:, slot, ts].unsqueeze(3).broadcast_to([P, GRP, 3, MUL, MUL]), ALU.mult).then_inc(prod_a, 1)

                def times_vectors(g):
                    ts = slice(g * GRP, g * GRP + GRP)
                    nc.vector.tensor_tensor(
                        prod[slot][:, ts, B:4 * B].rearrange("p t (i w u) -> p t i w u", i=3, w=MUL),
                        weights_of(g)[:, :, 3 * B:4 * B].rearrange("p t (w u) -> p t w u", w=MUL).unsqueeze(2).broadcast_to([P, GRP, 3, MUL, MUL]),
                        coef_v[:, slot, ts].unsqueeze(3).broadcast_to([P, GRP, 3, MUL, MUL]), ALU.mult).then_inc(prod_b, 1)

                def sum_over_u(g):
                    m, ts = n * NG + g, slice(g * GRP, g * GRP + GRP)
                    dve.wait_ge(prod_a, m + 1)
                    dve.wait_ge(prod_b, m + 1 + 2 * NG)
                    nc.vector.tensor_reduce(
                        prod[slot][:, ts, 0:3 * MUL], prod[slot][:, ts, 2 * B:5 * B].rearrange("p t (k u) -> p t k u", u=MUL),
                        AX.X, ALU.add).then_inc(reduced, 1)

                def times_sh1(g):
                    ts = slice(g * GRP, g * GRP + GRP)
                    dve.wait_ge(reduced, n * NG + g + 1)
                    nc.vector.tensor_tensor(
                        prod[slot][:, ts, 3 * MUL:6 * MUL].rearrange("p t (i w) -> p t i w", i=3),
                        prod[slot][:, ts, 2 * MUL:3 * MUL].unsqueeze(2).broadcast_to([P, GRP, 3, MUL]),
                        sh_sb[:, slot, ts, 1:4].unsqueeze(3).broadcast_to([P, GRP, 3, MUL]), ALU.mult).then_inc(feats, 1)

                vectors_by_sh1(0)
                sum_over_i(0)
                times_scalars(0)
                times_vectors(0)
                for g in range(1, NG):
                    vectors_by_sh1(g)
                    sum_over_u(g - 1)
                    sum_over_i(g)
                    times_sh1(g - 1)
                    times_scalars(g)
                    times_vectors(g)
                    if g == 1 and not is_early(s):
                        add_window(n - 2, before2)
                sum_over_u(NG - 1)
                if is_last(s):
                    before, here = window(s - 1), window(s)
                times_sh1(NG - 1)
                if is_last(s):
                    add_window(n - 1, before)
                    add_window(n, here)
            walk(dve, passes, products, at_end=next_windows(L1, 1))

            dve.wait_ge(self_used, 2 * NQ)
            for q in range(QB - 1):
                nc.vector.tensor_copy(quarters[q * F:(q + 1) * F], agg1[:, q * QN:(q + 1) * QN]).then_inc(quartered, 1)
            for b, js in enumerate(SUM_BLOCKS):
                got = ps[0:NP, b, 0:(js.stop - js.start) * P].rearrange("p (j q f) -> p q j f", q=QB, f=F)
                dve.wait_ge(summed, len(NORM_BLOCKS[1]) + b + 1)
                nc.vector.tensor_tensor(by_quarters(x_sb[0:NP])[:, :, js], got, by_quarters(lin_sb[0:NP])[:, :, js],
                                        ALU.add).then_inc(out_ready, 1)

        @block.tensor
        def _(pe):
            pe.sem_inc(L0.scattered, 2)
            pe.sem_inc(L1.scattered, 2 * NG)
            pe.sem_inc(tpw, 2 * NG)
            pe.sem_inc(combined, 1)
            pe.wait_ge(k_in, 16)
            pe.wait_ge(weights_in, 16 * NW)
            pe.wait_ge(w1_in, 16 * C)
            pe.wait_ge(consts_set, 1)

            def own_part(k):
                wt = w_self0 if k == 0 else w_self1

                def product(q):
                    pe.wait_ge(hT_ready, k * NQ + q + 1)
                    if k * NQ + q >= 2:
                        pe.wait_ge(self_used, k * NQ + q - 1)
                    nc.tensor.matmul(ps[0:NP, 2 + q % 2, 0:P], hT[:, q % 2], wt[:], start=True, stop=True).then_inc(self_ready, 1)

                pe.wait_ge(h_ready, BLOCKS_BEFORE[k + 1])
                for q in range(NQ):
                    if q >= 2:
                        pe.wait_ge(hT_ready, k * NQ + q - 1)
                    nc.tensor.transpose(ps[:, q % 2, 0:NP], h_sb[0:NP, q * QB:q * QB + QB].rearrange("p j f -> p (j f)"),
                                        k_sb[0:NP, K_ID:K_ID + NP]).then_inc(turned, 1)
                    if q >= 1:
                        product(q - 1)
                product(NQ - 1)

            own_part(0)
            pe.wait_ge(tables, 1)
            passes = pe.value_load(npass[0:1, 0:1], min_val=1, max_val=NWIN)
            pe.wait_ge(self_used, NQ)

            def turn_in(n, slot, use):
                pe.wait_ge(rad_in[slot], use * 16 + 16)
                nc.tensor.transpose(ps[0:C * NB, PS_IN, 384:512], rad_sb[:, slot], ident).then_inc(turned_in, 1)

            def hidden1(n, half):
                if half == 0:
                    pe.wait_ge(radT_done, n + 1)
                else:
                    pe.wait_ge(act1_done, n * 2 + 1)
                for q in range(3):
                    ins = nc.tensor.matmul(ps[:, PS_IN, q * P:q * P + P], w1_sb[:, half * 3 + q], radT, start=True, stop=True)
                ins.then_inc(hid1, 1)

            def hidden2(n, half):
                pe.wait_ge(act1_done, n * 2 + half + 1)
                pe.wait_ge(act2_done, n * 2 + half + 1)
                nc.tensor.matmul(ps[:, PS_H, 0:3 * P], w2_sb[:], act1[:, half].rearrange("p q e -> p (q e)"),
                                 start=True, stop=True).then_inc(hid2, 1)

            def sum_rows(r, n, s, slot, use, then):
                turn_in(n, slot, use)
                for half in range(2):
                    hidden1(n, half)
                    hidden2(n, half)
                pe.wait_ge(L0.onehot, n + 1)
                pe.wait_ge(L0.added, n + 1)
                for c in range(C):
                    if c % GRP == 0:
                        pe.wait_ge(L0.rows_in[slot][c // GRP], use * (16 * GRP) + 16 * GRP)
                    ins = nc.tensor.matmul(ps[64:128, slot, 0:W], rows[:, slot, c], onehot[:, slot, c],
                                           start=(c == 0), stop=(c == C - 1))
                ins.then_inc(L0.scattered, 1)
            walk(pe, passes, sum_rows, lambda r: pe.wait_ge(L0.opened, r + 1))

            pe.wait_ge(L0.opened, passes + 1)
            pe.wait_ge(act2_done, passes * (2 * S) + 1)
            for b, js in enumerate(NORM_BLOCKS[1]):
                for j in range(js.start, js.stop):
                    at = (j - js.start) * (F + 1)
                    ins = nc.tensor.matmul(ps[0:NP, b, at:at + F + 1], agg0[:, nodes_of(j)],
                                           w_mean[64:128], start=True, stop=True)
                ins.then_inc(summed, 1)
            pe.wait_ge(prep, 11)
            own_part(1)
            pe.wait_ge(self_used, 2 * NQ)
            pe.wait_ge(ones, 2)
            pe.wait_ge(consts_set, 3)

            def weights(n, g, slot, use):
                if g == 0:
                    pe.wait_ge(act2_in[slot], use * 16 + 16)
                for t in range(GRP):
                    tile = (g * GRP + t) * P
                    ins = nc.tensor.matmul(ps[:, 2 * g + t // 2, (t % 2) * NTP:(t % 2 + 1) * NTP],
                                           act2_1[:, slot, tile:tile + P], w3_sb[:], start=True, stop=True)
                ins.then_inc(tpw, 1)

            def scatter(n, g, slot):
                if g == 0:
                    pe.wait_ge(L1.onehot, n + 1)
                    pe.wait_ge(copied, n + 1)
                pe.wait_ge(feats, n * NG + g + 1 + 2 * NG)
                for c in range(g * GRP, g * GRP + GRP):
                    first = prod[slot][:, c, 0:1]
                    features = bass.AP(first.tensor, first.offset, [list(first.ap[0]), [5 * B, 2], [1, 2 * B]])
                    ins = nc.tensor.matmul(ps[0:W, PS_SUM, 0:4 * B], onehot[:, slot, c], features,
                                           start=(c == 0), stop=(c == C - 1))
                ins.then_inc(L1.scattered, 1)

            def turn_sums(n):
                pe.wait_ge(copied, n + 2)
                pe.wait_ge(L1.added, n + 1)
                for k in range(2):
                    ins = nc.tensor.transpose(ps[:, PS_TURN, k * P:(k + 1) * P], sums_sb[:, k * P:(k + 1) * P], ident)
                ins.then_inc(sums_turned, 1)

            def combine(n):
                pe.wait_ge(turned_copied, n + 1)
                for k, own in enumerate((1, 0)):
                    ins = nc.tensor.matmul(ps[0:F, PS_TURN, COMB:COMB + W], k_sb[:, K_COMB + own * F:K_COMB + own * F + F],
                                           turned_sb[:, k], start=(k == 0), stop=(k == 1))
                ins.then_inc(combined, 1)

            def start(r):
                pe.wait_ge(L1.opened, r + 1)
                weights(r * S, 0, 0, r * ((S + 1) // 2))
                weights(r * S, 1, 0, None)
                weights(r * S, 2, 0, None)

            def group_steps(r, n, s, slot, use, then):
                if not is_last(s):
                    pe.wait_ge(prod_b, n * NG + 3 * NG)
                    weights(n + 1, 0, 1 - slot, then)
                first = isinstance(s, int) and s == 0
                if not first:
                    turn_sums(n - 1)
                if not is_last(s):
                    weights(n + 1, 1, 1 - slot, None)
                scatter(n, 0, slot)
                if not first:
                    combine(n - 1)
                if not is_last(s):
                    weights(n + 1, 2, 1 - slot, None)
                scatter(n, 1, slot)
                scatter(n, 2, slot)
                if is_last(s):
                    turn_sums(n)
                    combine(n)
            walk(pe, passes, group_steps, start)

            pe.wait_ge(quartered, QB)
            for b, js in enumerate(SUM_BLOCKS):
                for j in range(js.start, js.stop):
                    at = (j - js.start) * P
                    ins = nc.tensor.transpose(ps[0:NP, b, at:at + P], quarters[:, nodes_of(j)], ident)
                ins.then_inc(summed, 1)


_INS = ['x', 'src', 'dst', 'edge_attr_4', 'edge_attr_8', 'L0_gnn_W', 'L0_gnn_b', 'L1_gnn_W1', 'L1_gnn_b1', 'L1_gnn_W2',
        'L1_gnn_b2', 'L1_gnn_W3', 'L1_gnn_b3', 'L1_gnn_Ws', 'L1_gnn_Wv']


def kernel(**inputs):
    import numpy as np
    import concourse.bacc as bacc
    from concourse.bass_utils import run_bass_kernel_spmd

    nc = bacc.Bacc("TRN2", target_bir_lowering=False, num_devices=1)
    arrays, args = {}, []
    for name in _INS:
        arrays[f"in_{name}"] = np.ascontiguousarray(inputs[name])
    arrays["in_constants"] = constants()
    for name, a in arrays.items():
        args.append(nc.dram_tensor(name, a.shape, mybir.dt.from_np(a.dtype), kind="ExternalInput").ap())
    args.append(nc.dram_tensor("out_x", (N, F), mybir.dt.float32, kind="ExternalOutput").ap())
    gnn(nc, *args)
    result = run_bass_kernel_spmd(nc, [arrays], core_ids=[0])
    return result.results[0]["out_x"]
```
